# Optimizing a Trainium2 kernel written in Bass

```python
import numpy as np
import jax
import jax.numpy as jnp

def _softmax(x, axis=-1):
    return jax.nn.softmax(x, axis=axis)

def _gelu(x):
    return jax.nn.gelu(x, approximate=True)

def _silu(x):
    return jax.nn.silu(x)

def _sigmoid(x):
    return jax.nn.sigmoid(x)

def _layernorm(x, axis=-1, eps=1e-05):
    m = jnp.mean(x, axis=axis, keepdims=True)
    v = jnp.var(x, axis=axis, keepdims=True)
    return (x - m) / jnp.sqrt(v + eps)

def _scatter_add(tgt, idx, src, axis=0):
    return tgt.at[idx].add(src)

def _segment_sum(src, seg, n):
    return jax.ops.segment_sum(src, seg, n)
kernel_name = 'mk_xattn_ffn_d1_seqx_r2_ddfa54'

def setup_inputs(seed: int=0):
    np.random.seed(seed)
    _w = jnp.asarray

    def _rec_inputs():
        import jax
        import jax.numpy as jnp
        _rk = jax.random.key(seed)
        x = -0.0002928 + 1 * jax.random.normal(jax.random.fold_in(_rk, 1), (2, 1024, 512), jnp.float32)
        _lenS = 1024 - jax.random.randint(jax.random.fold_in(_rk, 7), (2,), 0, max(1, 1024 // 4) + 1, jnp.int32)
        _lenS2 = 2048 - jax.random.randint(jax.random.fold_in(_rk, 8), (2,), 0, max(1, 2048 // 4) + 1, jnp.int32)
        _ctx_1024P = jax.random.normal(jax.random.fold_in(_rk, 11), (2, 16, 512), jnp.float32)
        _ctx_1024c = jax.random.dirichlet(jax.random.fold_in(_rk, 511), 0.3 * jnp.ones((16,), jnp.float32), (2, 2048))
        _ctx_1024t = jnp.einsum('bsk,bkd->bsd', _ctx_1024c, _ctx_1024P)
        _ctx_1024t = _ctx_1024t * jax.lax.rsqrt(jnp.mean(jnp.square(_ctx_1024t)) + 1e-12) * 0.953939
        ctx_1024 = -1.39393e-06 + 0.999914 * (_ctx_1024t + 0.3 * jax.random.normal(jax.random.fold_in(_rk, 611), (2, 2048, 512), jnp.float32))
        return (x, ctx_1024)
    x, ctx_1024 = _rec_inputs()

    def _L0_xattn_setup():
        import jax, jax.numpy as jnp
        import numpy as np
        EMBED_DIM = 512
        NUM_HEADS = 16
        HEAD_DIM = EMBED_DIM // NUM_HEADS
        SCALE = HEAD_DIM ** (-0.5)
        key = jax.random.key(seed)
        k1, k2, k3, k4, k5, k6 = jax.random.split(key, 6)
        B, Tq, Tk = (2, 1024, 1024)
        std = EMBED_DIM ** (-0.5)
        return {'x_q': jax.random.normal(k1, (B, Tq, EMBED_DIM), jnp.float32), 'x_kv': jax.random.normal(k2, (B, Tk, EMBED_DIM), jnp.float32), 'w_q': jax.random.normal(k3, (EMBED_DIM, EMBED_DIM), jnp.float32) * std, 'w_kv': jax.random.normal(k4, (EMBED_DIM, 2 * EMBED_DIM), jnp.float32) * std, 'w_proj': jax.random.normal(k5, (EMBED_DIM, EMBED_DIM), jnp.float32) * std, 'w_rel': jax.random.normal(k6, (1, NUM_HEADS), jnp.float32) * 0.02}
    _L0_xattn_all = _L0_xattn_setup()
    _L0_xattn_in = {k: v for k, v in _L0_xattn_all.items() if k in ('w_q', 'w_kv', 'w_proj', 'w_rel')}
    del _L0_xattn_all

    def _L0_ffn_setup():
        import jax, jax.numpy as jnp
        import numpy as np
        H = 8
        KD = 128
        TOPK = 8
        NUM_KEYS = 128
        N_EXPERTS = NUM_KEYS * NUM_KEYS
        N_DIM = 512
        BN_EPS = 1e-05

        def gelu_new(x):
            c = jnp.sqrt(jnp.asarray(2.0 / jnp.pi, x.dtype))
            return 0.5 * x * (1.0 + jnp.tanh(c * (x + 0.044715 * x * x * x)))
        key = jax.random.key(seed)
        ks = jax.random.split(key, 5)
        b, s = (2, 512)
        x = jax.random.normal(ks[0], (b, s, N_DIM), dtype=jnp.float32)
        w_q = jax.random.normal(ks[1], (N_DIM, 2 * H * KD), dtype=jnp.float32) * 0.02
        bn_gamma = jnp.ones((2 * H * KD,), dtype=jnp.float32)
        bn_beta = jnp.zeros((2 * H * KD,), dtype=jnp.float32)
        keys = jax.random.normal(ks[2], (H, NUM_KEYS, 2, KD), dtype=jnp.float32) * 0.02
        down_embed = jax.random.normal(ks[3], (N_EXPERTS, N_DIM), dtype=jnp.float32) * 0.02
        up_embed = jax.random.normal(ks[4], (N_EXPERTS, N_DIM), dtype=jnp.float32) * 0.02
        return {'x': x, 'w_q': w_q, 'bn_gamma': bn_gamma, 'bn_beta': bn_beta, 'keys': keys, 'down_embed': down_embed, 'up_embed': up_embed}
    _L0_ffn_all = _L0_ffn_setup()
    _L0_ffn_in = {k: v for k, v in _L0_ffn_all.items() if k in ('w_q', 'bn_gamma', 'bn_beta', 'keys', 'down_embed', 'up_embed')}
    del _L0_ffn_all
    return {'x': x, 'ctx_1024': ctx_1024, 'L0_xattn_w_q': _L0_xattn_in['w_q'], 'L0_xattn_w_kv': _L0_xattn_in['w_kv'], 'L0_xattn_w_proj': _L0_xattn_in['w_proj'], 'L0_xattn_w_rel': _L0_xattn_in['w_rel'], 'L0_ffn_w_q': _L0_ffn_in['w_q'], 'L0_ffn_bn_gamma': _L0_ffn_in['bn_gamma'], 'L0_ffn_bn_beta': _L0_ffn_in['bn_beta'], 'L0_ffn_keys': _L0_ffn_in['keys'], 'L0_ffn_down_embed': _L0_ffn_in['down_embed'], 'L0_ffn_up_embed': _L0_ffn_in['up_embed']}

def reference(x, ctx_1024, L0_xattn_w_q, L0_xattn_w_kv, L0_xattn_w_proj, L0_xattn_w_rel, L0_ffn_w_q, L0_ffn_bn_gamma, L0_ffn_bn_beta, L0_ffn_keys, L0_ffn_down_embed, L0_ffn_up_embed):
    import jax
    import jax.numpy as jnp

    def _L0_xattn_ref(x_q, x_kv, w_q, w_kv, w_proj, w_rel):
        import jax, jax.numpy as jnp
        import numpy as np
        EMBED_DIM = 512
        NUM_HEADS = 16
        HEAD_DIM = EMBED_DIM // NUM_HEADS
        SCALE = HEAD_DIM ** (-0.5)
        B, Tq, _ = x_q.shape
        Tk = x_kv.shape[1]
        q = x_q @ w_q
        kv = x_kv @ w_kv
        k, v = jnp.split(kv, 2, axis=-1)

        def heads(y, T):
            return y.reshape(B, T, NUM_HEADS, HEAD_DIM).transpose(0, 2, 1, 3)
        q = heads(q, Tq)
        k = heads(k, Tk)
        v = heads(v, Tk)
        logits = jnp.einsum('bhqd,bhkd->bhqk', q, k) * SCALE
        rel = jnp.arange(Tq, dtype=jnp.float32)[:, None] - jnp.arange(Tk, dtype=jnp.float32)[None, :]
        bias = rel[..., None] * w_rel[0]
        bias = bias.transpose(2, 0, 1)[None]
        logits = logits + bias
        attn = jax.nn.softmax(logits, axis=-1)
        out = jnp.einsum('bhqk,bhkd->bhqd', attn, v)
        out = out.transpose(0, 2, 1, 3).reshape(B, Tq, EMBED_DIM)
        return out @ w_proj

    def _L0_ffn_ref(x, w_q, bn_gamma, bn_beta, keys, down_embed, up_embed):
        import jax, jax.numpy as jnp
        import numpy as np
        H = 8
        KD = 128
        TOPK = 8
        NUM_KEYS = 128
        N_EXPERTS = NUM_KEYS * NUM_KEYS
        N_DIM = 512
        BN_EPS = 1e-05

        def gelu_new(x):
            c = jnp.sqrt(jnp.asarray(2.0 / jnp.pi, x.dtype))
            return 0.5 * x * (1.0 + jnp.tanh(c * (x + 0.044715 * x * x * x)))
        b, n, d = x.shape
        q = jnp.einsum('bnd,de->bne', x, w_q)
        mean = jnp.mean(q, axis=(0, 1))
        var = jnp.var(q, axis=(0, 1))
        q = (q - mean) * jax.lax.rsqrt(var + BN_EPS) * bn_gamma + bn_beta
        q = q.reshape(b, n, 2, H, KD).transpose(2, 0, 1, 3, 4)
        sim = jnp.einsum('pbnhd,hkpd->pbnhk', q, keys)
        sx, ix = jax.lax.top_k(sim[0], TOPK)
        sy, iy = jax.lax.top_k(sim[1], TOPK)
        all_scores = (sx[..., :, None] + sy[..., None, :]).reshape(b, n, H, TOPK * TOPK)
        all_indices = (ix[..., :, None] * NUM_KEYS + iy[..., None, :]).reshape(b, n, H, TOPK * TOPK)
        scores, pk = jax.lax.top_k(all_scores, TOPK)
        indices = jnp.take_along_axis(all_indices, pk, axis=-1)
        wd = down_embed[indices]
        wu = up_embed[indices]
        h = jnp.einsum('bnd,bnhkd->bnhk', x, wd)
        h = gelu_new(h)
        h = jax.nn.softmax(scores, axis=-1) * h
        out = jnp.einsum('bnhk,bnhkd->bnd', h, wu)
        return out
    x = x + _L0_xattn_ref(_layernorm(x, axis=-1), ctx_1024, L0_xattn_w_q, L0_xattn_w_kv, L0_xattn_w_proj, L0_xattn_w_rel)
    x = x + _L0_ffn_ref(_layernorm(x, axis=-1), L0_ffn_w_q, L0_ffn_bn_gamma, L0_ffn_bn_beta, L0_ffn_keys, L0_ffn_down_embed, L0_ffn_up_embed)
    return x

_drawn_inputs = setup_inputs


def setup_inputs(seed=0):
    import zlib

    import numpy as np

    out = dict(_drawn_inputs(seed))
    spreads = {'L0_ffn_bn_gamma': (1.0, 0.6), 'L0_ffn_bn_beta': (0.0, 0.8)}
    factors = {'L0_ffn_w_q': 8.0, 'L0_ffn_keys': 8.0, 'L0_ffn_down_embed': 8.0, 'L0_ffn_up_embed': 8.0}
    for name, (base, spread) in spreads.items():
        noise = np.random.default_rng([zlib.crc32(name.encode()), seed]).standard_normal(out[name].shape)
        drawn = base * np.exp(spread * noise) if base else spread * noise
        out[name] = jnp.asarray(drawn.astype(out[name].dtype))
    for name, factor in factors.items():
        out[name] = (out[name] * factor).astype(out[name].dtype)
    return out
```

```python
from contextlib import ExitStack

import concourse.bass as bass
from concourse import mybir

F32 = mybir.dt.float32
F32R = mybir.dt.float32r
U32 = mybir.dt.uint32
I32 = mybir.dt.int32
ALU = mybir.AluOpType
ACT = mybir.ActivationFunctionType
AX = mybir.AxisListType

P = 128
B, TQ, TK, D = 2, 1024, 2048, 512
H, DH = 16, 32
SCALE = DH ** -0.5
EPS = 1e-5
NHEAD = B * H
DC = D // P
CH = 512
TPC = CH // P
NT = B * TQ // P
QT = TQ // P
KT = TK // P
PH, KD, NKEY, TOPK = 8, 128, 128, 8
QC = 2 * PH
EW = 2 * D
NSLOT = PH * TOPK
GELU_C = (2.0 / 3.141592653589793) ** 0.5

BIAS0 = 3 * DH
MAX0 = BIAS0 + 4
KROWS = MAX0 + 2


def allocators(nc, ctx, tag):
    def sb(name, shape, dt=F32):
        return ctx.enter_context(nc.sbuf_tensor(f"{tag}_{name}", shape, dt))

    def psum(name, shape):
        return ctx.enter_context(nc.psum_tensor(f"{tag}_{name}", shape, F32))

    def sem(name):
        return ctx.enter_context(nc.semaphore(f"{tag}_{name}"))

    return sb, psum, sem


def gate(eng, passed):
    eng.sem_inc(passed, 1)


class Chain:

    def __init__(self, eng, sem, base=0):
        self.eng, self.sem, self.base, self.n = eng, sem, base, 0

    def mark(self, ins):
        ins.then_inc(self.sem, 1)
        self.n += 1

    def settle(self):
        self.eng.wait_ge(self.sem, self.base + self.n)

    def link(self, ins):
        self.mark(ins)
        self.settle()


def project(nc, x, ctx_t, w_q, w_kv, w_rel, ident_in, qa_d, ka_d, bq_d, v_all):
    with ExitStack() as ctx:
        sb, psum, sem = allocators(nc, ctx, "pj")
        NTURN = B * TQ // CH
        ident = sb("ident", [P, P])
        wkv = sb("wkv", [P, DC, 2 * D])
        wq = sb("wq", [P, DC, D])
        ct = [sb(f"ct{u}", [P, DC, CH]) for u in range(2)]
        xt = sb("xt", [P, TPC, D])
        xn = sb("xn", [P, TPC, D])
        xnt = sb("xnt", [P, DC, CH])
        hi = [sb(f"hi{u}", [P, CH]) for u in range(2)]
        lo = [sb(f"lo{u}", [P, CH]) for u in range(2)]
        stats = sb("stats", [P, TPC, 6])
        mv = sb("mv", [P, TPC, 2])
        sd = sb("sd", [P, TPC])
        rstd = sb("rstd", [P, TPC])
        nmr = sb("nmr", [P, TPC])
        eps = sb("eps", [P, 1])
        wr = sb("wr", [H, 1])
        ii = sb("ii", [H, TQ], I32)
        iw = sb("iw", [H, TQ])
        wrow = sb("wrow", [H, TQ])
        bq = sb("bq", [H, 4, TQ])
        acc = [psum(f"acc{u}", [P, CH]) for u in range(4)]
        tp = [psum(f"tp{u}", [P, CH]) for u in range(2)]

        consts_in = sem("consts_in")
        x_in = sem("x_in")
        ct_in = [sem(f"ct_in{u}") for u in range(2)]
        acc_full = sem("acc_full")
        acc_free = sem("acc_free")
        hi_done = sem("hi_done")
        out_done = [sem(f"out_done{u}") for u in range(2)]
        stats_done = sem("stats_done")
        sd_done = sem("sd_done")
        dve = sem("dve")
        scale_done = sem("scale_done")
        xn_done = sem("xn_done")
        tp_full = sem("tp_full")
        tp_free = sem("tp_free")
        iota_done = sem("iota_done")
        bias_done = sem("bias_done")
        bias_out = sem("bias_out")
        v_ones = sem("v_ones")
        eps_done = sem("eps_done")
        passed = sem("passed")

        plan = []
        for u in range(2):
            plan += [("k", u, e) for e in range(DC)] + [("v", u, s) for s in range(TPC)]
        plan += [("q", 0, e) for e in range(DC)]
        NPLAN = len(plan)
        split_at = [n for n, (kind, _, _) in enumerate(plan) if kind != "v"]
        NSPLIT = len(split_at)
        NV = NPLAN - NSPLIT

        block = ctx.enter_context(nc.Block())

        @block.sync
        def _(sp):
            sp.dma_start(wkv[:], w_kv.rearrange("(c p) e -> p c e", p=P)).then_inc(consts_in, 16)
            sp.dma_start(wq[:], w_q.rearrange("(c p) e -> p c e", p=P)).then_inc(consts_in, 16)
            sp.dma_start(ident[:], ident_in).then_inc(consts_in, 16)
            sp.dma_start(wr[:], w_rel.rearrange("o h -> h o")).then_inc(consts_in, 16)
            ctx_v = ctx_t.rearrange("(c p) t -> p c t", p=P)
            x_v = x.rearrange("b (n p) d -> p (b n) d", p=P)
            with sp.Fori(0, NTURN) as r:
                for u in range(2):
                    sp.wait_ge(acc_full, r * NPLAN)
                    sp.dma_start(ct[u][:], ctx_v[:, :, bass.ds(r * (2 * CH) + u * CH, CH)]).then_inc(ct_in[u], 16)
                sp.wait_ge(xn_done, r * TPC)
                sp.dma_start(xt[:], x_v[:, bass.ds(r * TPC, TPC), :]).then_inc(x_in, 16)
                for k, n in enumerate(split_at):
                    kind, u, e = plan[n]
                    sp.wait_ge(acc_free, r * NPLAN + n + 1)
                    dst, width = (ka_d, TK) if kind == "k" else (qa_d, TQ)
                    half = CH * (2 if kind == "k" else 1)
                    row = (r // 2) * D + e * P
                    col = (r & 1) * half + u * CH
                    sp.dma_start(dst[0, bass.ds(row, P), bass.ds(col, CH)], hi[k % 2][:]).then_inc(out_done[k % 2], 16)
                    sp.dma_start(dst[1, bass.ds(row, P), bass.ds(col, CH)], lo[k % 2][:]).then_inc(out_done[k % 2], 16)
            sp.wait_ge(bias_done, 1)
            sp.dma_start(bq_d, bq[:]).then_inc(bias_out, 16)
            sp.wait_ge(bias_out, 16)
            for u in range(2):
                sp.wait_ge(out_done[u], 32 * NTURN * NSPLIT // 2)

        @block.gpsimd
        def _(pool):
            pool.iota(ii[:], pattern=[[1, TQ]], base=0, channel_multiplier=0).then_inc(iota_done, 1)
            pool.memset(v_all[:, :, :, DH:DH + 1], 1.0).then_inc(v_ones, 1)

        @block.tensor
        def _(pe):
            pe.wait_ge(consts_in, 64)
            with pe.Fori(0, NTURN) as r:
                for n, (kind, u, part) in enumerate(plan):
                    if kind == "q" and part == 0:
                        for c in range(DC):
                            pe.wait_ge(xn_done, r * TPC + TPC)
                            if c >= 2:
                                pe.wait_ge(tp_free, r * DC + c - 1)
                            for s in range(TPC):
                                last = pe.transpose(tp[c % 2][:, s * P:(s + 1) * P], xn[:, s, c * P:(c + 1) * P], ident[:])
                            last.then_inc(tp_full, 1)
                        pe.wait_ge(tp_free, r * DC + DC)
                    if kind == "k" and part == 0:
                        pe.wait_ge(ct_in[u], r * 16 + 16)
                    bank = acc[n % 4]
                    if n >= 4:
                        pe.wait_ge(acc_free, r * NPLAN + n - 3)
                    for c in range(DC):
                        if kind == "k":
                            lhs, rhs = wkv[:, c, part * P:(part + 1) * P], ct[u][:, c, :]
                        elif kind == "v":
                            lhs, rhs = ct[u][:, c, part * P:(part + 1) * P], wkv[:, c, D:2 * D]
                        else:
                            lhs, rhs = wq[:, c, part * P:(part + 1) * P], xnt[:, c, :]
                        last = pe.matmul(bank[:], lhs, rhs, start=(c == 0), stop=(c == DC - 1))
                    last.then_inc(acc_full, 1)
                pe.wait_ge(acc_free, r * NPLAN + NPLAN)

        @block.scalar
        def _(act):
            act.wait_ge(eps_done, 1)
            with act.Fori(0, NTURN) as r:
                k = 0
                for n, (kind, u, part) in enumerate(plan):
                    if n == 4:
                        act.wait_ge(stats_done, r + 1)
                        act.activation(sd[:], mv[:, :, 1], ACT.Sqrt, bias=eps[:]).then_inc(sd_done, 1)
                    if n == 8:
                        act.wait_ge(scale_done, r + 1)
                        for s in range(TPC):
                            act.activation(xn[:, s, :], xt[:, s, :], ACT.Identity, bias=nmr[:, s:s + 1],
                                           scale=rstd[:, s:s + 1]).then_inc(xn_done, 1)
                    if kind == "q" and part == 0:
                        for c in range(DC):
                            act.wait_ge(tp_full, r * DC + c + 1)
                            act.activation(xnt[:, c, :], tp[c % 2][:], ACT.Copy).then_inc(tp_free, 1)
                    if kind == "v":
                        continue
                    act.wait_ge(acc_full, r * NPLAN + n + 1)
                    if k >= 2:
                        act.wait_ge(out_done[k % 2], r * (16 * NSPLIT) + 32 * (k // 2))
                    else:
                        act.wait_ge(out_done[k % 2], r * (16 * NSPLIT))
                    act.activation(hi[k % 2][:].bitcast(F32R), acc[n % 4][:], ACT.Copy,
                                   scale=(SCALE if kind == "q" else 1.0)).then_inc(hi_done, 1)
                    k += 1

        @block.vector
        def _(vec):
            chain = Chain(vec, dve)
            vec.memset(eps[:], EPS).then_inc(eps_done, 1)
            vec.wait_ge(iota_done, 1)
            vec.wait_ge(consts_in, 64)
            chain.link(vec.tensor_copy(iw[:], ii[:]))
            chain.link(vec.tensor_scalar(iw[:], iw[:], wr[:, 0:1], None, ALU.mult))
            chain.link(vec.tensor_scalar(wrow[:], iw[:], 0.0, wr[:, 0:1], ALU.mult, ALU.add))
            chain.link(vec.tensor_copy(bq[:, 0, :].bitcast(F32R), iw[:]))
            chain.link(vec.tensor_tensor(bq[:, 1, :].bitcast(F32R), iw[:], bq[:, 0, :], ALU.subtract))
            chain.link(vec.tensor_copy(bq[:, 2, :].bitcast(F32R), wrow[:]))
            vec.tensor_tensor(bq[:, 3, :].bitcast(F32R), wrow[:], bq[:, 2, :], ALU.subtract).then_inc(bias_done, 1)
            base = chain.n
            LINKS = 2
            vec.wait_ge(v_ones, 1)
            with vec.Fori(0, NTURN) as r:
                chain = Chain(vec, dve, r * LINKS + base)
                vec.wait_ge(x_in, r * 16 + 16)
                for s in range(TPC):
                    last = vec.bn_stats(stats[:, s, :], xt[:, s, :])
                chain.link(last)
                gate(vec, passed)
                for s in range(TPC):
                    last = vec.bn_aggr(mv[:, s, :], stats[:, s, :])
                last.then_inc(stats_done, 1)
                k = 0
                for n, (kind, u, part) in enumerate(plan):
                    if n == 4:
                        vec.wait_ge(sd_done, r + 1)
                        chain.link(vec.reciprocal(rstd[:], sd[:]))
                        vec.scalar_tensor_tensor(out=nmr[:], in0=mv[:, :, 0], scalar=-1.0, in1=rstd[:],
                                                 op0=ALU.mult, op1=ALU.mult).then_inc(scale_done, 1)
                    if kind == "v":
                        vec.wait_ge(acc_full, r * NPLAN + n + 1)
                        kt = (r & 1) * (KT // 2) + u * TPC + part
                        dst = v_all[:, bass.ds((r // 2) * H, H), bass.ds(kt, 1), 0:DH]
                        vec.tensor_copy(dst.rearrange("p h o d -> p (h o) d"),
                                        acc[n % 4][:].rearrange("p (h d) -> p h d", h=H)).then_inc(acc_free, 1)
                        continue
                    vec.wait_ge(hi_done, r * NSPLIT + k + 1)
                    vec.scalar_tensor_tensor(out=lo[k % 2][:].bitcast(F32R), in0=acc[n % 4][:],
                                             scalar=(SCALE if kind == "q" else 1.0), in1=hi[k % 2][:],
                                             op0=ALU.mult, op1=ALU.subtract).then_inc(acc_free, 1)
                    k += 1


def attend(nc, qa_d, ka_d, bq_d, m_d, v_all, ao, ident_in):
    with ExitStack() as ctx:
        sb, psum, sem = allocators(nc, ctx, "at")
        SLOTS, PB, HALF = 4, 4, TQ // 2
        KC = TK // CH
        NM = QT * KC
        ident = sb("ident", [P, P])
        qa = [sb(f"qa{u}", [P, TQ]) for u in range(SLOTS)]
        ka = [sb(f"ka{u}", [P, TK]) for u in range(SLOTS)]
        vs = [sb(f"vs{u}", [P, KT, DH + 1]) for u in range(SLOTS)]
        pb = [sb(f"pb{u}", [P, TQ]) for u in range(PB)]
        negj_i = sb("negj_i", [1, TK], I32)
        negj = sb("negj", [1, TK])
        mpart = sb("mpart", [P, QT, KC])
        mrow = sb("mrow", [P, QT])
        mx = sb("mx", [P, 2 * QT])
        mt = sb("mt", [2 * QT, P])
        rsum = sb("rsum", [P, QT])
        s_ps = [psum(f"s_ps{u}", [P, TQ]) for u in range(2)]
        m_ps = [psum(f"m_ps{u}", [P, CH]) for u in range(2)]
        o_ps = [psum(f"o_ps{u}", [P, CH]) for u in range(2)]

        ident_in_s = sem("ident_in")
        negj_made = sem("negj_made")
        negj_cast = sem("negj_cast")
        ones_made = sem("ones_made")
        rows_in = sem("rows_in")
        kq_in = [sem(f"kq_in{u}") for u in range(SLOTS)]
        v_copied = sem("v_copied")
        m_full = sem("m_full")
        m_free = sem("m_free")
        mx_made = sem("mx_made")
        mx_turned = sem("mx_turned")
        mt_made = sem("mt_made")
        mt_out = sem("mt_out")
        max_in = sem("max_in")
        s_full = sem("s_full")
        exp_done = sem("exp_done")
        av_done = sem("av_done")
        o_free = sem("o_free")
        passed = sem("passed")
        dve = sem("dve")
        LOADS = 7

        block = ctx.enter_context(nc.Block())

        @block.sync
        def _(sp):
            sp.dma_start(ident[:], ident_in).then_inc(ident_in_s, 16)
            sp.wait_ge(ones_made, SLOTS)
            sp.wait_ge(negj_cast, 1)
            for u in range(SLOTS):
                for k in range(2):
                    sp.dma_start(ka[u][BIAS0 + 2 + k:BIAS0 + 3 + k, :], negj[:]).then_inc(rows_in, 16)

            def load(i, u):
                for k, part in enumerate((0, 1, 0)):
                    sp.dma_start(ka[u][k * DH:(k + 1) * DH, :],
                                 ka_d[part, bass.ds(i * DH, DH), :]).then_inc(kq_in[u], 16)
                for k, part in enumerate((0, 0, 1)):
                    sp.dma_start(qa[u][k * DH:(k + 1) * DH, :],
                                 qa_d[part, bass.ds(i * DH, DH), :]).then_inc(kq_in[u], 16)
                src = bq_d[bass.ds(i & (H - 1), 1), :, :].rearrange("o r t -> (o r) t")
                sp.dma_start(qa[u][BIAS0:MAX0, :], src).then_inc(kq_in[u], 16)

            for u in range(SLOTS):
                load(u, u)
            with sp.Fori(1, NHEAD // SLOTS) as r:
                for u in range(SLOTS):
                    sp.wait_ge(av_done, r * (SLOTS * KT) + (u + 1 - SLOTS) * KT + PB)
                    load(r * SLOTS + u, u)

        @block.gpsimd
        def _(pool):
            pool.iota(negj_i[:], pattern=[[-1, TK]], base=0, channel_multiplier=0).then_inc(negj_made, 1)
            for u in range(SLOTS):
                pool.memset(ka[u][BIAS0:KROWS, :], 1.0).then_inc(ones_made, 1)
                pool.wait_ge(ones_made, u + 1)

            def head(i, u):
                pool.tensor_copy(vs[u][:].rearrange("p k d -> p (k d)"),
                                 v_all[:, bass.ds(i, 1), :, :].rearrange("p o k d -> p (o k d)")).then_inc(v_copied, 1)
                pool.wait_ge(mt_made, i + 1)
                gate(pool, passed)
                pool.dma_start(m_d[u].rearrange("a (b t) -> (a b) t", t=P), mt[:]).then_inc(mt_out, 16)
                pool.wait_ge(mt_out, i * 16 + 16)
                gate(pool, passed)
                pool.dma_start(qa[u][MAX0:KROWS, :], m_d[u]).then_inc(max_in, 16)

            for u in range(SLOTS):
                head(u, u)
            with pool.Fori(1, NHEAD // SLOTS) as r:
                for u in range(SLOTS):
                    pool.wait_ge(av_done, r * (SLOTS * KT) + (u + 1 - SLOTS) * KT + PB)
                    head(r * SLOTS + u, u)

        @block.tensor
        def _(pe):
            def maxima(i, u, a, b):
                for n in range(a, b):
                    qt, kc = n // KC, n % KC
                    if n == 0:
                        pe.wait_ge(kq_in[u], (i // SLOTS) * (16 * LOADS) + 16 * LOADS)
                    pe.wait_ge(m_free, i * NM + n + 1)
                    pe.matmul(m_ps[n % 2][:], qa[u][0:MAX0, qt * P:(qt + 1) * P].bitcast(F32R),
                              ka[u][0:MAX0, kc * CH:(kc + 1) * CH].bitcast(F32R),
                              start=True, stop=True).then_inc(m_full, 1)

            def turn_maxima(i, u):
                pe.wait_ge(mx_made, i + 1)
                pe.transpose(o_ps[u % 2][0:2 * QT, 0:P], mx[:], ident[:]).then_inc(mx_turned, 1)

            def scores(i, u, kt):
                if kt == 0:
                    pe.wait_ge(max_in, i * 16 + 16)
                pe.wait_ge(exp_done, i * KT + kt + 1)
                for h in range(2):
                    last = pe.matmul(s_ps[kt % 2][:, h * HALF:(h + 1) * HALF],
                                     ka[u][0:KROWS, kt * P:(kt + 1) * P].bitcast(F32R),
                                     qa[u][0:KROWS, h * HALF:(h + 1) * HALF].bitcast(F32R), start=True, stop=True)
                last.then_inc(s_full, 1)

            def values(j, u, kt):
                if kt == 0:
                    pe.wait_ge(v_copied, j + 1)
                    pe.wait_ge(o_free, j + 1)
                pe.wait_ge(exp_done, j * KT + kt + 3)
                for qt in range(QT):
                    last = pe.matmul(o_ps[u % 2][:, qt * (DH + 1):(qt + 1) * (DH + 1)],
                                     pb[kt % PB][:, qt * P:(qt + 1) * P], vs[u][:, kt, :],
                                     start=(kt == 0 and qt == 0), stop=(kt == KT - 1), skip_group_check=True)
                last.then_inc(av_done, 1)

            def head(j, u, last_head=False):
                un = (u + 1) % SLOTS
                i = j + 1
                for kt in range(KT):
                    if kt + 1 < KT:
                        scores(j, u, kt + 1)
                    if not last_head:
                        a, b = (min(NM, (5 * k + 1) // 2) for k in (kt, kt + 1))
                        maxima(i, un, a, b)
                        if kt == KT - 2:
                            turn_maxima(i, un)
                        if kt == KT - 1:
                            scores(i, un, 0)
                    values(j, u, kt)

            pe.wait_ge(ident_in_s, 16)
            pe.wait_ge(rows_in, 32 * SLOTS)
            maxima(0, 0, 0, NM)
            turn_maxima(0, 0)
            scores(0, 0, 0)
            with pe.Fori(0, NHEAD // SLOTS - 1) as r:
                for u in range(SLOTS):
                    head(r * SLOTS + u, u)
            for u in range(SLOTS):
                head(NHEAD - SLOTS + u, u, last_head=(u == SLOTS - 1))

        @block.scalar
        def _(act):
            act.nop().then_inc(exp_done, 2)
            with act.Fori(0, NHEAD) as j:
                for kt in range(KT):
                    act.wait_ge(s_full, j * KT + kt + 1)
                    act.wait_ge(av_done, j * KT + kt + 1)
                    act.activation(pb[kt % PB][:], s_ps[kt % 2][:], ACT.Exp).then_inc(exp_done, 1)

        @block.vector
        def _(vec):
            vec.nop().then_inc(m_free, 2)
            vec.nop().then_inc(av_done, PB)
            vec.nop().then_inc(o_free, 2)
            vec.wait_ge(negj_made, 1)
            vec.tensor_copy(negj[:].bitcast(F32R), negj_i[:]).then_inc(negj_cast, 1)

            def maxima(i, first, chain):
                for n in range(NM):
                    qt, kc = n // KC, n % KC
                    vec.wait_ge(m_full, i * NM + n + 1)
                    last = vec.tensor_reduce(mpart[:, qt, kc:kc + 1], m_ps[n % 2][:], AX.X, ALU.max)
                    last.then_inc(m_free, 1)
                vec.wait_ge(m_free, i * NM + NM + 2)
                chain.link(vec.tensor_reduce(mrow[:], mpart[:], AX.X, ALU.max))
                chain.link(vec.tensor_scalar(mx[:, 0:QT].bitcast(F32R), mrow[:], -1.0, None, ALU.mult))
                vec.scalar_tensor_tensor(out=mx[:, QT:2 * QT].bitcast(F32R), in0=mrow[:], scalar=-1.0,
                                         in1=mx[:, 0:QT], op0=ALU.mult, op1=ALU.subtract).then_inc(mx_made, 1)
                vec.wait_ge(mx_turned, i + 1)
                if not first:
                    vec.wait_ge(mt_out, i * 16)

            def turned(par):
                vec.tensor_copy(mt[:], o_ps[par][0:2 * QT, 0:P]).then_inc(mt_made, 1)

            def output(j, u, chain):
                vec.wait_ge(av_done, j * KT + KT + PB)
                vec.wait_ge(o_free, j + 2)
                o = o_ps[u % 2][:, 0:QT * (DH + 1)].rearrange("p (q d) -> p q d", q=QT)
                chain.link(vec.reciprocal(rsum[:], o[:, :, DH]))
                dst = ao[:, bass.ds(j, 1), :, :].rearrange("p o q d -> p (o q) d")
                vec.tensor_tensor(dst, o[:, :, 0:DH], rsum[:].unsqueeze(2).to_broadcast([P, QT, DH]),
                                  ALU.mult).then_inc(o_free, 1)

            chain = Chain(vec, dve)
            maxima(0, True, chain)
            turned(0)
            base = chain.n
            per = 3
            with vec.Fori(0, NHEAD // SLOTS - 1) as r:
                chain = Chain(vec, dve, r * (per * SLOTS) + base)
                for u in range(SLOTS):
                    maxima(r * SLOTS + u + 1, False, chain)
                    turned((u + 1) % 2)
                    output(r * SLOTS + u, u, chain)
            chain = Chain(vec, dve, (NHEAD - SLOTS) * per + base)
            for u in range(SLOTS):
                j = NHEAD - SLOTS + u
                if j + 1 < NHEAD:
                    maxima(j + 1, False, chain)
                    turned((u + 1) % 2)
                output(j, u, chain)


def mix(nc, x, w_proj, w_q, ident_in, ao, x2_d, xn_d, q_d, mvq):
    with ExitStack() as ctx:
        sb, psum, sem = allocators(nc, ctx, "mx")
        NCH = TQ // CH
        TT = NCH * TPC
        ident = sb("ident", [P, P])
        wp = sb("wp", [P, DC, D])
        wq = sb("wq", [P, DC, QC * P])
        xt = sb("xt", [P, TT, D])
        at = [sb(f"at{u}", [P, D]) for u in range(2)]
        att = [sb(f"att{u}", [P, D]) for u in range(2)]
        x2 = [sb(f"x2{u}", [P, D]) for u in range(2)]
        xn = [sb(f"xn{u}", [P, D]) for u in range(2)]
        xnt = [sb(f"xnt{u}", [P, DC, CH]) for u in range(2)]
        qs = [sb(f"qs{u}", [P, TPC, 4, P]) for u in range(4)]
        st = sb("st", [P, 6])
        mv = sb("mv", [P, 2])
        sd = sb("sd", [P, 1])
        rstd = sb("rstd", [P, 1])
        nmr = sb("nmr", [P, 1])
        eps = sb("eps", [P, 1])
        stq = sb("stq", [P, QC, NCH * B, 6])
        tp = [psum(f"tp{u}", [P, CH]) for u in range(2)]
        yp = [psum(f"yp{u}", [P, CH]) for u in range(2)]
        qp = [psum(f"qp{u}", [P, CH]) for u in range(4)]

        consts_in = sem("consts_in")
        x_in = sem("x_in")
        at_made = sem("at_made")
        at_turned = sem("at_turned")
        att_made = sem("att_made")
        y_full = sem("y_full")
        x2_made = sem("x2_made")
        stats_done = sem("stats_done")
        sd_done = sem("sd_done")
        scale_done = sem("scale_done")
        xn_made = sem("xn_made")
        xn_turned = sem("xn_turned")
        xnt_made = sem("xnt_made")
        q_full = sem("q_full")
        q_copied = sem("q_copied")
        q_counted = sem("q_counted")
        rows_out = [sem(f"rows_out{u}") for u in range(2)]
        q_out = [sem(f"q_out{u}") for u in range(4)]
        eps_done = sem("eps_done")
        passed = sem("passed")
        dve = sem("dve")
        NQ = NCH * QC

        block = ctx.enter_context(nc.Block())

        @block.sync
        def _(sp):
            sp.dma_start(ident[:], ident_in).then_inc(consts_in, 16)
            sp.dma_start(wp[:], w_proj.rearrange("(c p) e -> p c e", p=P)).then_inc(consts_in, 16)
            sp.dma_start(wq[:], w_q.rearrange("(c p) e -> p c e", p=P)).then_inc(consts_in, 16)
            x_v = x.rearrange("b (n p) d -> p (b n) d", p=P)
            with sp.Fori(0, B) as r:
                sp.wait_ge(x2_made, r * TT)
                sp.dma_start(xt[:], x_v[:, bass.ds(r * TT, TT), :]).then_inc(x_in, 16)
                def store_rows(t):
                    sp.wait_ge(xn_made, r * TT + t + 1)
                    sp.dma_start(x2_d[bass.ds(r * TQ + t * P, P), :], x2[t % 2][:]).then_inc(rows_out[t % 2], 16)
                    sp.dma_start(xn_d[bass.ds(r * TQ + t * P, P), :], xn[t % 2][:]).then_inc(rows_out[t % 2], 16)

                for t in range(TPC):
                    store_rows(t)
                for c in range(NCH):
                    for k in range(QC // 4):
                        if c + 1 < NCH:
                            store_rows((c + 1) * TPC + k)
                        sp.wait_ge(q_copied, r * NQ + c * QC + 4 * k + 4)
                        dst = q_d[bass.ds(r * TT + c * TPC, TPC), :, 4 * k:4 * k + 4, :]
                        sp.dma_start(dst.rearrange("s p k t -> p s (k t)"),
                                     qs[k][:].rearrange("p s k t -> p s (k t)")).then_inc(q_out[k], 16)
            for u in range(2):
                sp.wait_ge(rows_out[u], 32 * NT // 2)
            for u in range(4):
                sp.wait_ge(q_out[u], 16 * B * NCH)

        @block.gpsimd
        def _(pool):
            with pool.Fori(0, B) as r:
                for t in range(TT):
                    if t >= 2:
                        pool.wait_ge(at_turned, r * TT + t - 1)
                    else:
                        pool.wait_ge(at_turned, r * TT)
                    src = ao[:, bass.ds(r * H, H), t, :]
                    pool.tensor_copy(at[t % 2][:].rearrange("p (h d) -> p h d", h=H), src).then_inc(at_made, 1)

        @block.tensor
        def _(pe):
            pe.wait_ge(consts_in, 48)
            with pe.Fori(0, B) as r:
                def turn_attended(t):
                    pe.wait_ge(at_made, r * TT + t + 1)
                    pe.wait_ge(att_made, r * TT + t)
                    for c in range(DC):
                        last = pe.transpose(tp[0][:, c * P:(c + 1) * P], at[t % 2][:, c * P:(c + 1) * P], ident[:])
                    last.then_inc(at_turned, 1)

                def output(t):
                    pe.wait_ge(att_made, r * TT + t + 1)
                    pe.wait_ge(x2_made, r * TT + max(t - 1, 0))
                    for c in range(DC):
                        last = pe.matmul(yp[t % 2][:], att[t % 2][:, c * P:(c + 1) * P], wp[:, c, :],
                                         start=(c == 0), stop=(c == DC - 1))
                    last.then_inc(y_full, 1)

                def turn_normed(t):
                    pe.wait_ge(xn_made, r * TT + t + 1)
                    pe.wait_ge(xnt_made, r * TT + t)
                    for c in range(DC):
                        last = pe.transpose(tp[1][:, c * P:(c + 1) * P], xn[t % 2][:, c * P:(c + 1) * P], ident[:])
                    last.then_inc(xn_turned, 1)

                def queries(c, k):
                    n = c * QC + k
                    if k == 0:
                        pe.wait_ge(xnt_made, r * TT + (c + 1) * TPC)
                    if n >= 4:
                        pe.wait_ge(q_copied, r * NQ + n - 3)
                    else:
                        pe.wait_ge(q_copied, r * NQ)
                    for d in range(DC):
                        last = pe.matmul(qp[n % 4][:], wq[:, d, k * P:(k + 1) * P], xnt[c % 2][:, d, :],
                                         start=(d == 0), stop=(d == DC - 1))
                    last.then_inc(q_full, 1)

                def front(c, part):
                    t = c * TPC + part // 3
                    (turn_attended, output, turn_normed)[part % 3](t)

                for part in range(3 * TPC):
                    front(0, part)
                for k in range(QC):
                    queries(0, k)
                    if k < 3 * TPC:
                        front(1, k)
                for k in range(QC):
                    queries(1, k)

        @block.scalar
        def _(act):
            act.wait_ge(eps_done, 1)
            with act.Fori(0, B) as r:
                def copy_attended(t):
                    act.wait_ge(at_turned, r * TT + t + 1)
                    act.wait_ge(y_full, r * TT + max(t - 1, 0))
                    act.activation(att[t % 2][:], tp[0][:], ACT.Copy).then_inc(att_made, 1)

                def spread(t):
                    act.wait_ge(stats_done, r * TT + t + 1)
                    act.activation(sd[:], mv[:, 1:2], ACT.Sqrt, bias=eps[:]).then_inc(sd_done, 1)

                def copy_normed(t):
                    act.wait_ge(xn_turned, r * TT + t + 1)
                    c, s = divmod(t, TPC)
                    if s == 0:
                        act.wait_ge(q_full, r * NQ + max(c - 1, 0) * QC)
                    act.activation(xnt[c % 2][:, :, s * P:(s + 1) * P],
                                   tp[1][:].rearrange("p (c t) -> p c t", c=DC), ACT.Copy).then_inc(xnt_made, 1)

                def query(c, k):
                    n = c * QC + k
                    act.wait_ge(q_full, r * NQ + n + 1)
                    act.wait_ge(q_out[k // 4], r * (16 * NCH) + 16 * c)
                    act.wait_ge(q_counted, r * NQ + c * QC)
                    act.activation(qs[k // 4][:, :, k % 4, :], qp[n % 4][:].rearrange("p (s t) -> p s t", s=TPC),
                                   ACT.Copy).then_inc(q_copied, 1)

                def front(c, part):
                    t = c * TPC + part // 3
                    (copy_attended, spread, copy_normed)[part % 3](t)

                for part in range(3 * TPC):
                    front(0, part)
                for k in range(QC):
                    query(0, k)
                    if k < 3 * TPC:
                        front(1, k)
                for k in range(QC):
                    query(1, k)

        @block.vector
        def _(vec):
            vec.memset(eps[:], EPS).then_inc(eps_done, 1)
            LINKS = 2
            with vec.Fori(0, B) as r:
                chain = Chain(vec, dve, r * (LINKS * TT))
                vec.wait_ge(x_in, r * 16 + 16)

                def front(t):
                    vec.wait_ge(y_full, r * TT + t + 1)
                    vec.wait_ge(rows_out[t % 2], r * (16 * TT) + 32 * (t // 2))
                    vec.wait_ge(xn_turned, r * TT + max(t - 1, 0))
                    vec.tensor_tensor(x2[t % 2][:], yp[t % 2][:], xt[:, t, :], ALU.add).then_inc(x2_made, 1)
                    vec.wait_ge(x2_made, r * TT + t + 1)
                    chain.link(vec.bn_stats(st[:], x2[t % 2][:]))
                    gate(vec, passed)
                    vec.bn_aggr(mv[:], st[:]).then_inc(stats_done, 1)
                    vec.wait_ge(sd_done, r * TT + t + 1)
                    chain.link(vec.reciprocal(rstd[:], sd[:]))
                    vec.scalar_tensor_tensor(out=nmr[:], in0=mv[:, 0:1], scalar=-1.0, in1=rstd[:],
                                             op0=ALU.mult, op1=ALU.mult).then_inc(scale_done, 1)
                    vec.wait_ge(scale_done, r * TT + t + 1)
                    vec.tensor_scalar(xn[t % 2][:], x2[t % 2][:], rstd[:], nmr[:], ALU.mult,
                                      ALU.add).then_inc(xn_made, 1)

                def query(c, k):
                    vec.wait_ge(q_copied, r * NQ + c * QC + k + 1)
                    g = r * NCH + c
                    vec.bn_stats(stq[:, k, bass.ds(g, 1), :].rearrange("p o s -> p (o s)"),
                                 qs[k // 4][:, :, k % 4, :]).then_inc(q_counted, 1)

                for t in range(TPC):
                    front(t)
                for k in range(QC):
                    query(0, k)
                    if k < 3 * TPC and k % 3 == 1:
                        front(TPC + k // 3)
                for k in range(QC):
                    query(1, k)
            vec.wait_ge(q_counted, B * NQ)
            for k in range(QC):
                vec.bn_aggr(mvq[:, k, :], stq[:, k, :, :].rearrange("p g s -> p (g s)"))


def experts(nc, table, keys_t, gamma_t, beta_t, ident_in, mvq, x2_d, xn_d, q_d, out):
    with ExitStack() as ctx:
        sb, psum, sem = allocators(nc, ctx, "ex")
        RG = 4
        ident = sb("ident", [P, P])
        keys = sb("keys", [P, QC, NKEY])
        gam = sb("gam", [P, QC])
        bet = sb("bet", [P, QC])
        eps = sb("eps", [P, 1])
        qsc = sb("qsc", [P, QC])
        qbi = sb("qbi", [P, QC])
        qt = sb("qt", [P, QC, P])
        qn = sb("qn", [P, QC, P])
        xn = [sb(f"xn{u}", [P, D]) for u in range(2)]
        x2 = [sb(f"x2{u}", [P, D]) for u in range(2)]
        yo = sb("yo", [P, D])
        ring = [sb(f"ring{g}", [P, TOPK, EW]) for g in range(RG)]
        diag = [sb(f"diag{k}", [P, P]) for k in range(TOPK)]
        eight_i = sb("eight_i", [P, TOPK], I32)
        eight = sb("eight", [P, TOPK])
        top = sb("top", [P, QC, TOPK])
        pos = sb("pos", [P, QC, TOPK], U32)
        posf = sb("posf", [P, QC, TOPK])
        cand = sb("cand", [P, PH, TOPK * TOPK])
        best = sb("best", [P, PH, TOPK])
        pick = sb("pick", [P, 2, NSLOT], U32)
        pickf = sb("pickf", [P, 2, NSLOT])
        hot = sb("hot", [P, NSLOT, TOPK])
        sel = sb("sel", [P, 2, NSLOT])
        idx = [sb(f"idx{u}", [P, NSLOT], U32) for u in range(2)]
        shifted = sb("shifted", [P, PH, TOPK])
        expd = sb("expd", [P, PH, TOPK])
        esum = sb("esum", [P, PH])
        wgt = [sb(f"wgt{u}", [P, PH, TOPK]) for u in range(2)]
        hid = sb("hid", [P, TOPK])
        g1 = sb("g1", [P, TOPK])
        g2 = sb("g2", [P, TOPK])
        g3 = sb("g3", [P, TOPK])
        g4 = sb("g4", [P, TOPK])
        wh = sb("wh", [P, TOPK])
        coef = sb("coef", [P, TOPK])
        sim = [psum(f"sim{u}", [P, 4, NKEY]) for u in range(4)]
        acc = [psum(f"acc{u}", [P, D]) for u in range(2)]

        consts_in = sem("consts_in")
        q_in = sem("q_in")
        x_in = [sem(f"x_in{u}") for u in range(2)]
        qn_made = sem("qn_made")
        sim_made = sem("sim_made")
        sim_read = sem("sim_read")
        shift_made = sem("shift_made")
        exp_made = sem("exp_made")
        routed = sem("routed")
        rows_in = [sem(f"rows_in{g}") for g in range(RG)]
        arg_made = sem("arg_made")
        gelu_exp = sem("gelu_exp")
        coef_made = sem("coef_made")
        diag_made = sem("diag_made")
        diag_used = sem("diag_used")
        y_made = sem("y_made")
        y_out = sem("y_out")
        qsd_made = sem("qsd_made")
        aff_made = sem("aff_made")
        eight_made = sem("eight_made")
        passed = sem("passed")
        mv_ready = sem("mv_ready")
        dve = sem("dve")

        ROUTE_LINKS = 17
        GROUP_LINKS = TOPK + 6
        TILE_LINKS = ROUTE_LINKS + PH * GROUP_LINKS

        block = ctx.enter_context(nc.Block())

        @block.sync
        def _(sp):
            sp.dma_start(ident[:], ident_in).then_inc(consts_in, 16)
            sp.dma_start(keys[:], keys_t).then_inc(consts_in, 16)
            sp.dma_start(gam[:], gamma_t).then_inc(consts_in, 16)
            sp.dma_start(bet[:], beta_t).then_inc(consts_in, 16)

            def load(t, u):
                sp.dma_start(qt[:].rearrange("p c t -> p (c t)"),
                             q_d[bass.ds(t, 1), :, :, :].rearrange("o p c t -> (o p) (c t)")).then_inc(q_in, 16)
                sp.dma_start(xn[u][:], xn_d[bass.ds(t * P, P), :]).then_inc(x_in[u], 16)
                sp.dma_start(x2[u][:], x2_d[bass.ds(t * P, P), :]).then_inc(x_in[u], 16)

            def tile(t, u):
                sp.wait_ge(qn_made, t * QC + QC)
                if u == 1:
                    sp.wait_ge(y_made, t)
                else:
                    sp.wait_ge(y_made, t)
                load(t + 1, 1 - u)

            def store(t):
                sp.wait_ge(y_made, t + 1)
                sp.dma_start(out[bass.ds(t * P, P), :], yo[:]).then_inc(y_out, 16)

            load(0, 0)
            with sp.Fori(0, NT // 2 - 1) as r:
                for u in range(2):
                    tile(r * 2 + u, u)
                    store(r * 2 + u)
            tile(NT - 2, 0)
            store(NT - 2)
            store(NT - 1)
            sp.wait_ge(y_out, 16 * NT)

        @block.gpsimd
        def _(pool):
            pool.iota(eight_i[:], pattern=[[1, TOPK]], base=0, channel_multiplier=0).then_inc(eight_made, 1)
            with pool.Fori(0, NT // 2) as r:
                for u in range(2):
                    pool.wait_ge(routed, r * 2 + u + 1)
                    for g in range(PH):
                        pool.wait_ge(diag_used, r * (2 * PH) + u * PH + g + 1)
                        gate(pool, passed)
                        for k in range(TOPK):
                            n = g * TOPK + k
                            pool.indirect_dma_start(
                                ring[g % RG][:, k, :], None, table,
                                bass.IndirectOffsetOnAxis(ap=idx[u][:, n:n + 1], axis=0),
                            ).then_inc(rows_in[g % RG], 16)

        @block.tensor
        def _(pe):
            pe.wait_ge(consts_in, 64)

            def similar(t):
                pe.wait_ge(sim_read, t)
                for c in range(QC):
                    pe.wait_ge(qn_made, t * QC + c + 1)
                    last = pe.matmul(sim[c // 4][:, c % 4, :], qn[:, c, :], keys[:, c, :], start=True, stop=True)
                last.then_inc(sim_made, 1)

            def group(t, u, g):
                if g == 0:
                    pe.wait_ge(y_made, max(t - 1, 0) if isinstance(t, int) else t - 1)
                pe.wait_ge(rows_in[g % RG], t * (PH // RG * TOPK * 16) + (g // RG + 1) * TOPK * 16)
                for k in range(TOPK):
                    pe.wait_ge(diag_made, t * NSLOT + g * TOPK + k + 1)
                    last = pe.matmul(acc[u][:], diag[k][:], ring[g % RG][:, k, D:EW],
                                     start=(g == 0 and k == 0), stop=(g == PH - 1 and k == TOPK - 1))
                last.then_inc(diag_used, 1)

            def tile(t, u, routes=True):
                for g in range(PH):
                    if g == 3 and routes:
                        similar(t + 1)
                    group(t, u, g)

            similar(0)
            for u in range(2):
                tile(u, u)
            with pe.Fori(1, NT // 2 - 1) as r:
                for u in range(2):
                    tile(r * 2 + u, u)
            tile(NT - 2, 0)
            tile(NT - 1, 1, routes=False)

        @block.scalar
        def _(act):
            act.wait_ge(aff_made, 1)
            act.activation(qsc[:], mvq[:, :, 1], ACT.Sqrt, bias=eps[:]).then_inc(qsd_made, 1)
            act.wait_ge(aff_made, 2)

            def affine(t):
                act.wait_ge(q_in, t * 16 + 16)
                act.wait_ge(sim_made, t)
                for c in range(QC):
                    act.activation(qn[:, c, :], qt[:, c, :], ACT.Identity, bias=qbi[:, c:c + 1],
                                   scale=qsc[:, c:c + 1]).then_inc(qn_made, 1)

            def weights(t):
                act.wait_ge(shift_made, t + 1)
                act.activation(expd[:], shifted[:], ACT.Exp).then_inc(exp_made, 1)

            def group(t, g):
                n = t * PH + g
                act.wait_ge(arg_made, n + 1)
                act.activation(g4[:], g3[:], ACT.Exp).then_inc(gelu_exp, 1)
                act.wait_ge(coef_made, n + 1)
                act.wait_ge(diag_used, n + RG)
                for k in range(TOPK):
                    act.activation(diag[k][:], ident[:], ACT.Copy, scale=coef[:, k:k + 1]).then_inc(diag_made, 1)

            def tile(t, routes=True):
                for g in range(PH):
                    if g == 2 and routes:
                        affine(t + 1)
                    group(t, g)
                    if g == 3 and routes:
                        weights(t + 1)

            act.wait_ge(consts_in, 64)
            affine(0)
            weights(0)
            with act.Fori(0, NT - 1) as t:
                tile(t)
            tile(NT - 1, routes=False)

        @block.vector
        def _(vec):
            chain = Chain(vec, dve)
            vec.nop().then_inc(diag_used, RG)
            chain.mark(vec.memset(eps[:], EPS))
            chain.settle()
            vec.nop().then_inc(aff_made, 1)
            vec.wait_ge(eight_made, 1)
            vec.wait_ge(consts_in, 64)
            chain.mark(vec.tensor_copy(eight[:], eight_i[:]))
            vec.wait_ge(qsd_made, 1)
            chain.link(vec.reciprocal(qbi[:], qsc[:]))
            chain.link(vec.tensor_tensor(qsc[:], qbi[:], gam[:], ALU.mult))
            chain.link(vec.tensor_tensor(qbi[:], mvq[:, :, 0], qsc[:], ALU.mult))
            vec.tensor_tensor(qbi[:], bet[:], qbi[:], ALU.subtract).then_inc(aff_made, 1)

            def route(t, u, chain):
                start = chain.n
                vec.wait_ge(sim_made, t + 1)
                gate(vec, passed)
                for c in range(QC):
                    last = vec.max(top[:, c, :], sim[c // 4][:, c % 4, :])
                chain.link(last)
                gate(vec, passed)
                for c in range(QC):
                    last = vec.max_index(pos[:, c, :], top[:, c, :], sim[c // 4][:, c % 4, :])
                last.then_inc(sim_read, 1)
                vec.wait_ge(sim_read, t + 1)
                chain.mark(vec.tensor_copy(posf[:], pos[:]))
                pair = [P, PH, TOPK, TOPK]
                chain.link(vec.tensor_tensor(cand[:].rearrange("p h (a b) -> p h a b", a=TOPK),
                                             top[:, 0:PH, :].unsqueeze(3).to_broadcast(pair),
                                             top[:, PH:QC, :].unsqueeze(2).to_broadcast(pair), ALU.add))
                gate(vec, passed)
                for h in range(PH):
                    last = vec.max(best[:, h, :], cand[:, h, :])
                chain.link(last)
                gate(vec, passed)
                for h in range(PH):
                    last = vec.max_index(pick[:, 0, h * TOPK:(h + 1) * TOPK], best[:, h, :], cand[:, h, :])
                chain.link(last)
                vec.tensor_tensor(shifted[:], best[:], best[:, :, 0:1].to_broadcast([P, PH, TOPK]),
                                  ALU.subtract).then_inc(shift_made, 1)
                chain.link(vec.tensor_scalar(pick[:, 1, :], pick[:, 0, :], 7, None, ALU.bitwise_and))
                chain.link(vec.tensor_scalar(pick[:, 0, :], pick[:, 0, :], 3, None, ALU.logical_shift_right))
                chain.link(vec.tensor_copy(pickf[:], pick[:]))
                for side in range(2):
                    chain.link(vec.tensor_tensor(
                        hot[:], pickf[:, side, :].unsqueeze(2).to_broadcast([P, NSLOT, TOPK]),
                        eight[:].unsqueeze(1).to_broadcast([P, NSLOT, TOPK]), ALU.is_equal))
                    hot4 = hot[:].rearrange("p (h k) a -> p h k a", h=PH)
                    chain.link(vec.tensor_tensor(
                        hot4, hot4, posf[:, side * PH:(side + 1) * PH, :].unsqueeze(2).to_broadcast(pair), ALU.mult))
                    chain.link(vec.tensor_reduce(sel[:, side, :], hot[:], AX.X, ALU.add))
                vec.scalar_tensor_tensor(out=idx[u][:], in0=sel[:, 0, :], scalar=float(NKEY), in1=sel[:, 1, :],
                                         op0=ALU.mult, op1=ALU.add).then_inc(routed, 1)
                vec.wait_ge(exp_made, t + 1)
                chain.link(vec.tensor_reduce(esum[:], expd[:], AX.X, ALU.add))
                chain.link(vec.reciprocal(esum[:], esum[:]))
                chain.mark(vec.tensor_tensor(wgt[u][:], expd[:], esum[:].unsqueeze(2).to_broadcast([P, PH, TOPK]),
                                             ALU.mult))
                assert chain.n == start + ROUTE_LINKS

            def group(t, u, g, chain):
                start = chain.n
                if g == 0:
                    vec.wait_ge(x_in[u], (t // 2) * 32 + 32)
                vec.wait_ge(rows_in[g % RG], t * (PH // RG * TOPK * 16) + (g // RG + 1) * TOPK * 16)
                for k in range(TOPK):
                    down = ring[g % RG][:, k, 0:D]
                    chain.mark(vec.tensor_tensor_reduce(down, down, xn[u][:], 1.0, 0.0,
                                                        ALU.mult, ALU.add, hid[:, k:k + 1]))
                chain.settle()
                chain.link(vec.tensor_tensor(g1[:], hid[:], hid[:], ALU.mult))
                chain.link(vec.tensor_scalar(g2[:], g1[:], -2 * GELU_C * 0.044715, -2 * GELU_C, ALU.mult, ALU.add))
                chain.link(vec.tensor_tensor(g1[:], g2[:], hid[:], ALU.mult))
                vec.tensor_scalar(g3[:], g1[:], 80.0, None, ALU.min).then_inc(arg_made, 1)
                chain.link(vec.tensor_tensor(wh[:], hid[:], wgt[u][:, g, :], ALU.mult))
                vec.wait_ge(gelu_exp, t * PH + g + 1)
                chain.link(vec.tensor_scalar(g2[:], g4[:], 1.0, None, ALU.add))
                chain.link(vec.reciprocal(g2[:], g2[:]))
                vec.wait_ge(diag_made, t * NSLOT + g * TOPK)
                vec.tensor_tensor(coef[:], wh[:], g2[:], ALU.mult).then_inc(coef_made, 1)
                assert chain.n == start + GROUP_LINKS

            def finish(t, u):
                vec.wait_ge(diag_used, t * PH + PH + RG)
                vec.wait_ge(y_out, t * 16)
                vec.tensor_tensor(yo[:], acc[u][:], x2[u][:], ALU.add).then_inc(y_made, 1)

            def tile(t, u, chain, routes=True):
                for g in range(PH):
                    group(t, u, g, chain)
                    if g == 3 and routes:
                        route(t + 1, 1 - u, chain)
                finish(t, u)

            route(0, 0, chain)
            base = chain.n
            with vec.Fori(0, NT // 2 - 1) as r:
                chain = Chain(vec, dve, r * (2 * TILE_LINKS) + base)
                for u in range(2):
                    tile(r * 2 + u, u, chain)
            chain = Chain(vec, dve, (NT - 2) * TILE_LINKS + base)
            tile(NT - 2, 0, chain)
            tile(NT - 1, 1, chain, routes=False)


def program(nc, x, ctx_t, w_q, w_kv, w_proj, w_rel, f_wq, gamma_t, beta_t, keys_t, table, ident, out):
    with ExitStack() as ctx:
        def dram(name, shape):
            return nc.dram_tensor(name, shape, F32, kind="Internal").ap()

        qa_d = dram("qa_d", [2, NHEAD * DH, TQ])
        ka_d = dram("ka_d", [2, NHEAD * DH, TK])
        bq_d = dram("bq_d", [H, 4, TQ])
        m_d = dram("m_d", [4, 2, TQ])
        x2_d = dram("x2_d", [B * TQ, D])
        xn_d = dram("xn_d", [B * TQ, D])
        q_d = dram("q_d", [NT, P, QC, P])
        mvq = ctx.enter_context(nc.sbuf_tensor("mvq", [P, QC, 2], F32))
        with ExitStack() as attention:
            ao = attention.enter_context(nc.sbuf_tensor("ao", [P, NHEAD, QT, DH], F32))
            with ExitStack() as values:
                v_all = values.enter_context(nc.sbuf_tensor("v_all", [P, NHEAD, KT, DH + 1], F32))
                project(nc, x, ctx_t, w_q, w_kv, w_rel, ident, qa_d, ka_d, bq_d, v_all)
                attend(nc, qa_d, ka_d, bq_d, m_d, v_all, ao, ident)
            mix(nc, x, w_proj, f_wq, ident, ao, x2_d, xn_d, q_d, mvq)
        experts(nc, table, keys_t, gamma_t, beta_t, ident, mvq, x2_d, xn_d, q_d, out)


def kernel(**inputs):
    import numpy as np
    import concourse.bacc as bacc
    from concourse.bass_utils import run_bass_kernel_spmd

    a = {k: np.asarray(v) for k, v in inputs.items()}
    c = np.ascontiguousarray
    arrays = {
        "x": a["x"],
        "ctx_t": c(a["ctx_1024"].reshape(B * TK, D).T),
        "w_q": a["L0_xattn_w_q"],
        "w_kv": a["L0_xattn_w_kv"],
        "w_proj": a["L0_xattn_w_proj"],
        "w_rel": a["L0_xattn_w_rel"],
        "f_wq": a["L0_ffn_w_q"],
        "gamma_t": c(a["L0_ffn_bn_gamma"].reshape(QC, P).T),
        "beta_t": c(a["L0_ffn_bn_beta"].reshape(QC, P).T),
        "keys_t": c(a["L0_ffn_keys"].transpose(3, 2, 0, 1).reshape(KD, QC, NKEY)),
        "table": np.concatenate([a["L0_ffn_down_embed"], a["L0_ffn_up_embed"]], axis=1),
        "ident": np.eye(P, dtype=np.float32),
    }
    nc = bacc.Bacc("TRN2", target_bir_lowering=False, num_devices=1)
    aps = [nc.dram_tensor(n, v.shape, mybir.dt.from_np(v.dtype), kind="ExternalInput").ap() for n, v in arrays.items()]
    out = nc.dram_tensor("out", [B * TQ, D], F32, kind="ExternalOutput").ap()
    program(nc, *aps, out)
    r = run_bass_kernel_spmd(nc, [arrays], core_ids=[0])
    return r.results[0]["out"].reshape(B, TQ, D)
```

```python
from contextlib import ExitStack

import concourse.bass as bass
from concourse import mybir

F32 = mybir.dt.float32
F32R = mybir.dt.float32r
U32 = mybir.dt.uint32
I32 = mybir.dt.int32
ALU = mybir.AluOpType
ACT = mybir.ActivationFunctionType
AX = mybir.AxisListType

P = 128
B, TQ, TK, D = 2, 1024, 2048, 512
H, DH = 16, 32
SCALE = DH ** -0.5
EPS = 1e-5
NHEAD = B * H
DC = D // P
CH = 512
TPC = CH // P
NT = B * TQ // P
QT = TQ // P
KT = TK // P
PH, KD, NKEY, TOPK = 8, 128, 128, 8
QC = 2 * PH
EW = 2 * D
NSLOT = PH * TOPK
GELU_C = (2.0 / 3.141592653589793) ** 0.5

BIAS0 = 3 * DH
MAX0 = BIAS0 + 4
KROWS = MAX0 + 2


def allocators(nc, ctx, tag):
    def sb(name, shape, dt=F32):
        return ctx.enter_context(nc.sbuf_tensor(f"{tag}_{name}", shape, dt))

    def psum(name, shape):
        return ctx.enter_context(nc.psum_tensor(f"{tag}_{name}", shape, F32))

    def sem(name):
        return ctx.enter_context(nc.semaphore(f"{tag}_{name}"))

    return sb, psum, sem


def gate(eng, passed):
    eng.sem_inc(passed, 1)


class Chain:

    def __init__(self, eng, sem, base=0):
        self.eng, self.sem, self.base, self.n = eng, sem, base, 0

    def mark(self, ins):
        ins.then_inc(self.sem, 1)
        self.n += 1

    def settle(self):
        self.eng.wait_ge(self.sem, self.base + self.n)

    def link(self, ins):
        self.mark(ins)
        self.settle()


def project(nc, x, ctx_t, w_q, w_kv, w_rel, ident_in, qa_d, ka_d, bq_d, v_all):
    with ExitStack() as ctx:
        sb, psum, sem = allocators(nc, ctx, "pj")
        NTURN = B * TQ // CH
        ident = sb("ident", [P, P])
        wkv = sb("wkv", [P, DC, 2 * D])
        wq = sb("wq", [P, DC, D])
        ct = [sb(f"ct{u}", [P, DC, CH]) for u in range(2)]
        xt = sb("xt", [P, TPC, D])
        xn = sb("xn", [P, TPC, D])
        xnt = sb("xnt", [P, DC, CH])
        hi = [sb(f"hi{u}", [P, CH]) for u in range(2)]
        lo = [sb(f"lo{u}", [P, CH]) for u in range(2)]
        stats = sb("stats", [P, TPC, 6])
        mv = sb("mv", [P, TPC, 2])
        sd = sb("sd", [P, TPC])
        rstd = sb("rstd", [P, TPC])
        nmr = sb("nmr", [P, TPC])
        eps = sb("eps", [P, 1])
        wr = sb("wr", [H, 1])
        ii = sb("ii", [H, TQ], I32)
        iw = sb("iw", [H, TQ])
        wrow = sb("wrow", [H, TQ])
        bq = sb("bq", [H, 4, TQ])
        acc = [psum(f"acc{u}", [P, CH]) for u in range(4)]
        tp = [psum(f"tp{u}", [P, CH]) for u in range(2)]

        consts_in = sem("consts_in")
        x_in = sem("x_in")
        ct_in = [sem(f"ct_in{u}") for u in range(2)]
        acc_full = sem("acc_full")
        acc_free = sem("acc_free")
        hi_done = sem("hi_done")
        out_done = [sem(f"out_done{u}") for u in range(2)]
        stats_done = sem("stats_done")
        sd_done = sem("sd_done")
        dve = sem("dve")
        scale_done = sem("scale_done")
        xn_done = sem("xn_done")
        tp_full = sem("tp_full")
        tp_free = sem("tp_free")
        iota_done = sem("iota_done")
        bias_done = sem("bias_done")
        bias_out = sem("bias_out")
        eps_done = sem("eps_done")
        passed = sem("passed")

        plan = []
        for u in range(2):
            plan += [("k", u, e) for e in range(DC)] + [("v", u, s) for s in range(TPC)]
        plan += [("q", 0, e) for e in range(DC)]
        NPLAN = len(plan)
        split_at = [n for n, (kind, _, _) in enumerate(plan) if kind != "v"]
        NSPLIT = len(split_at)
        NV = NPLAN - NSPLIT

        block = ctx.enter_context(nc.Block())

        @block.sync
        def _(sp):
            sp.dma_start(wkv[:], w_kv.rearrange("(c p) e -> p c e", p=P)).then_inc(consts_in, 16)
            sp.dma_start(wq[:], w_q.rearrange("(c p) e -> p c e", p=P)).then_inc(consts_in, 16)
            sp.dma_start(ident[:], ident_in).then_inc(consts_in, 16)
            sp.dma_start(wr[:], w_rel.rearrange("o h -> h o")).then_inc(consts_in, 16)
            ctx_v = ctx_t.rearrange("(c p) t -> p c t", p=P)
            x_v = x.rearrange("b (n p) d -> p (b n) d", p=P)
            with sp.Fori(0, NTURN) as r:
                for u in range(2):
                    sp.wait_ge(acc_full, r * NPLAN)
                    sp.dma_start(ct[u][:], ctx_v[:, :, bass.ds(r * (2 * CH) + u * CH, CH)]).then_inc(ct_in[u], 16)
                sp.wait_ge(xn_done, r * TPC)
                sp.dma_start(xt[:], x_v[:, bass.ds(r * TPC, TPC), :]).then_inc(x_in, 16)
                for k, n in enumerate(split_at):
                    kind, u, e = plan[n]
                    sp.wait_ge(acc_free, r * NPLAN + n + 1)
                    dst, width = (ka_d, TK) if kind == "k" else (qa_d, TQ)
                    half = CH * (2 if kind == "k" else 1)
                    row = (r // 2) * D + e * P
                    col = (r & 1) * half + u * CH
                    sp.dma_start(dst[0, bass.ds(row, P), bass.ds(col, CH)], hi[k % 2][:]).then_inc(out_done[k % 2], 16)
                    sp.dma_start(dst[1, bass.ds(row, P), bass.ds(col, CH)], lo[k % 2][:]).then_inc(out_done[k % 2], 16)
            sp.wait_ge(bias_done, 1)
            sp.dma_start(bq_d, bq[:]).then_inc(bias_out, 16)
            sp.wait_ge(bias_out, 16)
            for u in range(2):
                sp.wait_ge(out_done[u], 32 * NTURN * NSPLIT // 2)

        @block.gpsimd
        def _(pool):
            pool.iota(ii[:], pattern=[[1, TQ]], base=0, channel_multiplier=0).then_inc(iota_done, 1)

        @block.tensor
        def _(pe):
            pe.wait_ge(consts_in, 64)
            with pe.Fori(0, NTURN) as r:
                for n, (kind, u, part) in enumerate(plan):
                    if kind == "q" and part == 0:
                        for c in range(DC):
                            pe.wait_ge(xn_done, r * TPC + TPC)
                            if c >= 2:
                                pe.wait_ge(tp_free, r * DC + c - 1)
                            for s in range(TPC):
                                last = pe.transpose(tp[c % 2][:, s * P:(s + 1) * P], xn[:, s, c * P:(c + 1) * P], ident[:])
                            last.then_inc(tp_full, 1)
                        pe.wait_ge(tp_free, r * DC + DC)
                    if kind == "k" and part == 0:
                        pe.wait_ge(ct_in[u], r * 16 + 16)
                    bank = acc[n % 4]
                    if n >= 4:
                        pe.wait_ge(acc_free, r * NPLAN + n - 3)
                    for c in range(DC):
                        if kind == "k":
                            lhs, rhs = wkv[:, c, part * P:(part + 1) * P], ct[u][:, c, :]
                        elif kind == "v":
                            lhs, rhs = ct[u][:, c, part * P:(part + 1) * P], wkv[:, c, D:2 * D]
                        else:
                            lhs, rhs = wq[:, c, part * P:(part + 1) * P], xnt[:, c, :]
                        last = pe.matmul(bank[:], lhs, rhs, start=(c == 0), stop=(c == DC - 1))
                    last.then_inc(acc_full, 1)
                pe.wait_ge(acc_free, r * NPLAN + NPLAN)

        @block.scalar
        def _(act):
            act.wait_ge(eps_done, 1)
            with act.Fori(0, NTURN) as r:
                k = 0
                for n, (kind, u, part) in enumerate(plan):
                    if n == 4:
                        act.wait_ge(stats_done, r + 1)
                        act.activation(sd[:], mv[:, :, 1], ACT.Sqrt, bias=eps[:]).then_inc(sd_done, 1)
                    if n == 8:
                        act.wait_ge(scale_done, r + 1)
                        for s in range(TPC):
                            act.activation(xn[:, s, :], xt[:, s, :], ACT.Identity, bias=nmr[:, s:s + 1],
                                           scale=rstd[:, s:s + 1]).then_inc(xn_done, 1)
                    if kind == "q" and part == 0:
                        for c in range(DC):
                            act.wait_ge(tp_full, r * DC + c + 1)
                            act.activation(xnt[:, c, :], tp[c % 2][:], ACT.Copy).then_inc(tp_free, 1)
                    if kind == "v":
                        continue
                    act.wait_ge(acc_full, r * NPLAN + n + 1)
                    if k >= 2:
                        act.wait_ge(out_done[k % 2], r * (16 * NSPLIT) + 32 * (k // 2))
                    else:
                        act.wait_ge(out_done[k % 2], r * (16 * NSPLIT))
                    act.activation(hi[k % 2][:].bitcast(F32R), acc[n % 4][:], ACT.Copy,
                                   scale=(SCALE if kind == "q" else 1.0)).then_inc(hi_done, 1)
                    k += 1

        @block.vector
        def _(vec):
            chain = Chain(vec, dve)
            vec.memset(eps[:], EPS).then_inc(eps_done, 1)
            vec.wait_ge(iota_done, 1)
            vec.wait_ge(consts_in, 64)
            chain.link(vec.tensor_copy(iw[:], ii[:]))
            chain.link(vec.tensor_scalar(iw[:], iw[:], wr[:, 0:1], None, ALU.mult))
            chain.link(vec.tensor_scalar(wrow[:], iw[:], 0.0, wr[:, 0:1], ALU.mult, ALU.add))
            chain.link(vec.tensor_copy(bq[:, 0, :].bitcast(F32R), iw[:]))
            chain.link(vec.tensor_tensor(bq[:, 1, :].bitcast(F32R), iw[:], bq[:, 0, :], ALU.subtract))
            chain.link(vec.tensor_copy(bq[:, 2, :].bitcast(F32R), wrow[:]))
            vec.tensor_tensor(bq[:, 3, :].bitcast(F32R), wrow[:], bq[:, 2, :], ALU.subtract).then_inc(bias_done, 1)
            base = chain.n
            LINKS = 2
            with vec.Fori(0, NTURN) as r:
                chain = Chain(vec, dve, r * LINKS + base)
                vec.wait_ge(x_in, r * 16 + 16)
                for s in range(TPC):
                    last = vec.bn_stats(stats[:, s, :], xt[:, s, :])
                chain.link(last)
                gate(vec, passed)
                for s in range(TPC):
                    last = vec.bn_aggr(mv[:, s, :], stats[:, s, :])
                last.then_inc(stats_done, 1)
                k = 0
                for n, (kind, u, part) in enumerate(plan):
                    if n == 4:
                        vec.wait_ge(sd_done, r + 1)
                        chain.link(vec.reciprocal(rstd[:], sd[:]))
                        vec.scalar_tensor_tensor(out=nmr[:], in0=mv[:, :, 0], scalar=-1.0, in1=rstd[:],
                                                 op0=ALU.mult, op1=ALU.mult).then_inc(scale_done, 1)
                    if kind == "v":
                        vec.wait_ge(acc_full, r * NPLAN + n + 1)
                        kt = (r & 1) * (KT // 2) + u * TPC + part
                        dst = v_all[:, bass.ds((r // 2) * H, H), bass.ds(kt, 1), :]
                        vec.tensor_copy(dst.rearrange("p h o d -> p (h o) d"),
                                        acc[n % 4][:].rearrange("p (h d) -> p h d", h=H)).then_inc(acc_free, 1)
                        continue
                    vec.wait_ge(hi_done, r * NSPLIT + k + 1)
                    vec.scalar_tensor_tensor(out=lo[k % 2][:].bitcast(F32R), in0=acc[n % 4][:],
                                             scalar=(SCALE if kind == "q" else 1.0), in1=hi[k % 2][:],
                                             op0=ALU.mult, op1=ALU.subtract).then_inc(acc_free, 1)
                    k += 1


def attend(nc, qa_d, ka_d, bq_d, m_d, v_all, ao, ident_in):
    with ExitStack() as ctx:
        sb, psum, sem = allocators(nc, ctx, "at")
        SLOTS = 4
        UNROLL = SLOTS
        HALF = TQ // 2
        STEPS = 2 * KT // 2
        HSTEPS = STEPS // 2
        LAG = 3
        PB = 4
        KC = TK // CH
        NM = QT * KC
        VW = 2 * DH + 1
        HQ = HALF // P
        SPLIT = 416
        TURN_MAX, COPY_OUT, TURN_OUT = 1, 3, 5
        MAKE_V = 6
        VALUES_AT = 1
        ident = sb("ident", [P, P])
        qa = [sb(f"qa{u}", [P, TQ]) for u in range(SLOTS)]
        ka = [sb(f"ka{u}", [P, TK]) for u in range(SLOTS)]
        vs = [sb(f"vs{u}", [P, KT, VW]) for u in range(2)]
        pf = [sb(f"pf{u}", [P, 2 * HALF]) for u in range(2)]
        ph = [sb(f"ph{u}", [P, 2 * HALF]) for u in range(PB)]
        pl = [sb(f"pl{u}", [P, 2 * HALF]) for u in range(PB)]
        ot = [sb(f"ot{u}", [VW, HALF]) for u in range(2)]
        negj_int = sb("negj_int", [KT, P], I32)
        negj = sb("negj", [KT, P])
        mpart = sb("mpart", [P, QT, KC])
        mrow = sb("mrow", [P, QT])
        mx = sb("mx", [P, 2 * QT])
        mt = sb("mt", [2 * QT, P])
        rsum = sb("rsum", [P, HQ])
        osum = sb("osum", [P, HQ, DH])
        s_ps = [psum(f"s_ps{u}", [P, 2 * HALF]) for u in range(2)]
        m_ps = [psum(f"m_ps{u}", [P, CH]) for u in range(2)]
        o_ps = [psum(f"o_ps{u}", [P, HALF]) for u in range(2)]

        ident_in_s = sem("ident_in")
        negj_made = sem("negj_made")
        negj_cast = sem("negj_cast")
        negj_out = sem("negj_out")
        ones_made = sem("ones_made")
        rows_in = sem("rows_in")
        kq_in = [sem(f"kq_in{u}") for u in range(SLOTS)]
        v_hi = sem("v_hi")
        v_made = sem("v_made")
        m_full = sem("m_full")
        m_free = sem("m_free")
        mx_made = sem("mx_made")
        mt_made = sem("mt_made")
        mt_out = sem("mt_out")
        max_in = sem("max_in")
        s_full = sem("s_full")
        exp_done = sem("exp_done")
        hi_done = sem("hi_done")
        lo_vec = sem("lo_vec")
        lo_pool = sem("lo_pool")
        av_done = sem("av_done")
        ot_made = sem("ot_made")
        dve = sem("dve")
        passed = sem("passed")
        LOADS = 7

        def uses(u, n, first, last):
            for k in range(2 * n, 2 * n + 2):
                if not last or u < UNROLL - 2:
                    yield "max", k
            if n == TURN_MAX and not (last and u == UNROLL - 1):
                yield "turn", 0
            if n == TURN_OUT and not (first and u == 0):
                yield "out", 1
            if n == TURN_OUT + HSTEPS:
                yield "out", 0

        class Ring:

            def __init__(self, base, parity):
                self.base, self.parity, self.n = base, parity, 0

            def next(self):
                self.n += 1
                return self.base + self.n, (self.parity + self.n - 1) % 2

        BEFORE = 2 * NM + 1
        FIRST = BEFORE + sum(len(list(uses(u, n, True, False))) for u in range(UNROLL) for n in range(STEPS))
        TURN = sum(len(list(uses(u, n, False, False))) for u in range(UNROLL) for n in range(STEPS))
        assert TURN % 2 == 0
        NTURN = NHEAD // UNROLL

        block = ctx.enter_context(nc.Block())

        @block.sync
        def _(sp):
            sp.dma_start(ident[:], ident_in).then_inc(ident_in_s, 16)
            sp.wait_ge(ones_made, SLOTS)
            sp.wait_ge(negj_cast, 1)
            sp.dma_start(m_d[0].rearrange("a (b t) -> (a b) t", t=P), negj[:]).then_inc(negj_out, 16)
            sp.wait_ge(negj_out, 16)
            for u in range(SLOTS):
                for k in range(2):
                    sp.dma_start(ka[u][BIAS0 + 2 + k:BIAS0 + 3 + k, :],
                                 m_d[0].rearrange("a t -> (a t)").rearrange("(o t) -> o t", o=1)).then_inc(rows_in, 16)

            def load(i, u):
                for k, part in enumerate((0, 1, 0)):
                    sp.dma_start(ka[u][k * DH:(k + 1) * DH, :],
                                 ka_d[part, bass.ds(i * DH, DH), :]).then_inc(kq_in[u], 16)
                for k, part in enumerate((0, 0, 1)):
                    sp.dma_start(qa[u][k * DH:(k + 1) * DH, :],
                                 qa_d[part, bass.ds(i * DH, DH), :]).then_inc(kq_in[u], 16)
                src = bq_d[bass.ds(i & (H - 1), 1), :, :].rearrange("o r t -> (o r) t")
                sp.dma_start(qa[u][BIAS0:MAX0, :], src).then_inc(kq_in[u], 16)

            def move_maxima(i, u):
                sp.wait_ge(mt_made, i + 1)
                sp.dma_start(m_d[u].rearrange("a (b t) -> (a b) t", t=P), mt[:]).then_inc(mt_out, 16)
                sp.wait_ge(mt_out, i * 16 + 16)
                sp.dma_start(qa[u][MAX0:KROWS, :], m_d[u]).then_inc(max_in, 16)

            for u in range(SLOTS):
                load(u, u)
            sp.wait_ge(rows_in, 32 * SLOTS)
            move_maxima(0, 0)
            with sp.Fori(0, NTURN - 1) as r:
                for u in range(SLOTS):
                    move_maxima(r * SLOTS + u + 1, (u + 1) % SLOTS)
                    sp.wait_ge(av_done, r * (SLOTS * STEPS) + (u + 1) * STEPS + PB)
                    load(r * SLOTS + u + SLOTS, u)
            for u in range(1, SLOTS):
                move_maxima(NHEAD - SLOTS + u, u)

        @block.gpsimd
        def _(pool):
            pool.iota(negj_int[:], pattern=[[-1, P]], base=0, channel_multiplier=-P).then_inc(negj_made, 1)
            for u in range(SLOTS):
                pool.memset(ka[u][BIAS0:KROWS, :], 1.0).then_inc(ones_made, 1)
                pool.wait_ge(ones_made, u + 1)
            for u in range(2):
                pool.memset(vs[u][:, :, 2 * DH:VW], 1.0).then_inc(ones_made, 1)
                pool.wait_ge(ones_made, SLOTS + u + 1)

            def make_v_hi(i, u):
                pool.tensor_copy(vs[u % 2][:, :, 0:DH].bitcast(F32R),
                                 v_all[:, bass.ds(i, 1), :, :].rearrange("p o k d -> p (o k) d")).then_inc(v_hi, 1)

            def make_v_lo(i, u):
                pool.wait_ge(v_hi, i + 1)
                gate(pool, passed)
                pool.tensor_tensor(vs[u % 2][:, :, DH:2 * DH].bitcast(F32R),
                                   v_all[:, bass.ds(i, 1), :, :].rearrange("p o k d -> p (o k) d"),
                                   vs[u % 2][:, :, 0:DH], ALU.subtract).then_inc(v_made, 1)

            def head(j, u, last):
                for n in range(STEPS):
                    N = j * STEPS + n
                    pool.wait_ge(hi_done, N + 3)
                    pool.tensor_tensor(pl[n % PB][:, SPLIT:].bitcast(F32R), pf[n % 2][:, SPLIT:],
                                       ph[n % PB][:, SPLIT:], ALU.subtract).then_inc(lo_pool, 1)
                    if last:
                        continue
                    if n == MAKE_V:
                        pool.wait_ge(av_done, j * STEPS + PB)
                        make_v_hi(j + 1, u + 1)
                    if n == MAKE_V + 1:
                        make_v_lo(j + 1, u + 1)

            make_v_hi(0, 0)
            make_v_lo(0, 0)
            with pool.Fori(0, NTURN - 1) as r:
                for u in range(UNROLL):
                    head(r * UNROLL + u, u, False)
            for u in range(UNROLL):
                head(NHEAD - UNROLL + u, u, u == UNROLL - 1)

        @block.tensor
        def _(pe):
            def maximum(i, u, k, use, bank):
                qt, kc = k // KC, k % KC
                if k == 0:
                    pe.wait_ge(kq_in[u], (i // SLOTS) * (16 * LOADS) + 16 * LOADS)
                pe.wait_ge(m_free, use)
                pe.matmul(m_ps[bank][:], qa[u][0:MAX0, qt * P:(qt + 1) * P].bitcast(F32R),
                          ka[u][0:MAX0, kc * CH:(kc + 1) * CH].bitcast(F32R),
                          start=True, stop=True).then_inc(m_full, 1)

            def turn_maxima(i, use, bank):
                pe.wait_ge(mx_made, i + 1)
                pe.wait_ge(m_free, use)
                pe.transpose(m_ps[bank][0:2 * QT, 0:P], mx[:], ident[:]).then_inc(m_full, 1)

            def turn_output(j, h, use, bank):
                pe.wait_ge(ot_made, j * 2 + h + 3)
                pe.wait_ge(m_free, use)
                for q in range(HQ):
                    last = pe.transpose(m_ps[bank][:, q * VW:(q + 1) * VW], ot[h][:, q * P:(q + 1) * P],
                                        ident[0:VW, 0:VW])
                last.then_inc(m_full, 1)

            def scores(j, u, n):
                h, kp = divmod(n, HSTEPS)
                if n == 0:
                    pe.wait_ge(max_in, j * 16 + 16)
                pe.wait_ge(hi_done, j * STEPS + n + 1)
                for k in range(2):
                    kt = 2 * kp + k
                    last = pe.matmul(s_ps[n % 2][:, k * HALF:(k + 1) * HALF],
                                     ka[u][0:KROWS, kt * P:(kt + 1) * P].bitcast(F32R),
                                     qa[u][0:KROWS, h * HALF:(h + 1) * HALF].bitcast(F32R), start=True, stop=True)
                last.then_inc(s_full, 1)

            def values(j, u, n):
                h, kp = divmod(n, HSTEPS)
                if n == 0:
                    pe.wait_ge(v_made, j + 1)
                if kp == 0:
                    pe.wait_ge(ot_made, j * 2 + h + 1)
                pe.wait_ge(lo_vec, j * STEPS + n + 3)
                pe.wait_ge(lo_pool, j * STEPS + n + 3)
                for k in range(2):
                    for part in (ph, pl):
                        last = pe.matmul(o_ps[h][0:VW, :], vs[u % 2][:, 2 * kp + k, :].bitcast(F32R),
                                         part[n % PB][:, k * HALF:(k + 1) * HALF].bitcast(F32R),
                                         start=(kp == 0 and k == 0 and part is ph),
                                         stop=(kp == HSTEPS - 1 and k == 1 and part is pl))
                last.then_inc(av_done, 1)

            def lagged(j, u, n):
                if isinstance(j, int) and j * STEPS + n < LAG:
                    return
                values(*((j, u, n - LAG) if n >= LAG else (j - 1, (u - 1) % UNROLL, n - LAG + STEPS)))

            def head(j, u, ring, first=False, last=False):
                for n in range(STEPS):
                    scores(j, u, n)
                    for pos, (kind, k) in enumerate(uses(u, n, first, last)):
                        if pos == VALUES_AT:
                            lagged(j, u, n)
                        if kind == "max":
                            maximum(j + 2, (u + 2) % SLOTS, k, *ring.next())
                        elif kind == "turn":
                            turn_maxima(j + 1, *ring.next())
                        else:
                            turn_output(j - k, k, *ring.next())
                    if len(list(uses(u, n, first, last))) <= VALUES_AT:
                        lagged(j, u, n)

            pe.wait_ge(ident_in_s, 16)
            pe.wait_ge(rows_in, 32 * SLOTS)
            ring = Ring(0, 0)
            for i in range(2):
                for k in range(NM):
                    maximum(i, i, k, *ring.next())
                if i == 0:
                    turn_maxima(0, *ring.next())
            for u in range(UNROLL):
                head(u, u, ring, first=True)
            assert ring.n == FIRST
            with pe.Fori(1, NTURN - 1) as r:
                ring = Ring(r * TURN + (FIRST - TURN), FIRST % 2)
                for u in range(UNROLL):
                    head(r * UNROLL + u, u, ring)
            ring = Ring(FIRST + (NTURN - 2) * TURN, FIRST % 2)
            for u in range(UNROLL):
                head(NHEAD - UNROLL + u, u, ring, last=True)
            for n in range(STEPS - LAG, STEPS):
                values(NHEAD - 1, UNROLL - 1, n)
            turn_output(NHEAD - 1, 1, *ring.next())

        @block.scalar
        def _(act):
            act.nop().then_inc(hi_done, 2)
            act.nop().then_inc(ot_made, 2)

            def copy_output(j, h):
                act.wait_ge(av_done, j * STEPS + (h + 1) * HSTEPS + PB)
                act.activation(ot[h][:], o_ps[h][0:VW, :], ACT.Copy).then_inc(ot_made, 1)

            def head(j, u, first=False):
                for n in range(STEPS):
                    N = j * STEPS + n
                    act.wait_ge(s_full, N + 1)
                    act.wait_ge(lo_vec, N + 1)
                    act.wait_ge(lo_pool, N + 1)
                    act.activation(pf[n % 2][:], s_ps[n % 2][:], ACT.Exp).then_inc(exp_done, 1)
                    act.wait_ge(av_done, N + 1)
                    act.activation(ph[n % PB][:].bitcast(F32R), s_ps[n % 2][:], ACT.Exp).then_inc(hi_done, 1)
                    if n == COPY_OUT and not (first and u == 0):
                        copy_output(j - 1, 1)
                    if n == COPY_OUT + HSTEPS:
                        copy_output(j, 0)

            for u in range(UNROLL):
                head(u, u, first=True)
            with act.Fori(1, NTURN) as r:
                for u in range(UNROLL):
                    head(r * UNROLL + u, u)
            copy_output(NHEAD - 1, 1)

        @block.vector
        def _(vec):
            vec.nop().then_inc(m_free, 2)
            vec.nop().then_inc(av_done, PB)
            vec.nop().then_inc(lo_vec, 2)
            vec.nop().then_inc(lo_pool, 2)
            vec.wait_ge(negj_made, 1)
            vec.tensor_copy(negj[:].bitcast(F32R), negj_int[:]).then_inc(negj_cast, 1)

            def maximum(k, use, bank):
                vec.wait_ge(m_full, use)
                vec.tensor_reduce(mpart[:, k // KC, k % KC:k % KC + 1], m_ps[bank][:], AX.X, ALU.max)\
                   .then_inc(m_free, 1)

            def make_mx(use, chain):
                vec.wait_ge(m_free, use + 2)
                chain.link(vec.tensor_reduce(mrow[:], mpart[:], AX.X, ALU.max))
                chain.link(vec.tensor_scalar(mx[:, 0:QT].bitcast(F32R), mrow[:], -1.0, None, ALU.mult))
                vec.scalar_tensor_tensor(out=mx[:, QT:2 * QT].bitcast(F32R), in0=mrow[:], scalar=-1.0,
                                         in1=mx[:, 0:QT], op0=ALU.mult, op1=ALU.subtract).then_inc(mx_made, 1)

            def copy_maxima(i, use, bank, any_before=True):
                vec.wait_ge(m_full, use)
                if any_before:
                    vec.wait_ge(mt_out, i * 16)
                vec.tensor_copy(mt[:], m_ps[bank][0:2 * QT, 0:P]).then_inc(m_free, 1)
                vec.wait_ge(m_free, use + 2)
                vec.sem_inc(mt_made, 1)

            def output(j, h, use, bank, chain):
                vec.wait_ge(m_full, use)
                o = m_ps[bank][:, 0:HQ * VW].rearrange("p (q d) -> p q d", q=HQ)
                chain.mark(vec.tensor_copy(osum[:], o[:, :, DH:2 * DH]))
                chain.link(vec.reciprocal(rsum[:], o[:, :, 2 * DH]))
                chain.link(vec.tensor_tensor(osum[:], osum[:], o[:, :, 0:DH], ALU.add))
                dst = ao[:, bass.ds(j, 1), h * HQ:(h + 1) * HQ, :].rearrange("p o q d -> p (o q) d")
                vec.tensor_tensor(dst, osum[:], rsum[:].unsqueeze(2).to_broadcast([P, HQ, DH]),
                                  ALU.mult).then_inc(m_free, 1)
                vec.wait_ge(m_free, use + 2)

            def low(j, n):
                vec.wait_ge(hi_done, j * STEPS + n + 3)
                vec.tensor_tensor(pl[n % PB][:, 0:SPLIT].bitcast(F32R), pf[n % 2][:, 0:SPLIT],
                                  ph[n % PB][:, 0:SPLIT], ALU.subtract).then_inc(lo_vec, 1)

            def head(j, u, ring, chain, first=False, last=False):
                for n in range(STEPS):
                    for kind, k in uses(u, n, first, last):
                        use, bank = ring.next()
                        if kind == "max":
                            maximum(k, use, bank)
                            if k % 2 == 0 and not (first and u == 0 and n == 0):
                                low(*((j, n - 1) if n else (j - 1, STEPS - 1)))
                            if k == NM - 1:
                                make_mx(use, chain)
                        elif kind == "turn":
                            copy_maxima(j + 1, use, bank)
                        else:
                            output(j - k, k, use, bank, chain)
                    if last and u >= UNROLL - 2:
                        low(*((j, n - 1) if n else (j - 1, STEPS - 1)))

            chain = Chain(vec, dve)
            ring = Ring(0, 0)
            for i in range(2):
                for k in range(NM):
                    use, bank = ring.next()
                    maximum(k, use, bank)
                make_mx(use, chain)
                if i == 0:
                    copy_maxima(0, *ring.next(), any_before=False)
            for u in range(UNROLL):
                head(u, u, ring, chain, first=True)
            base = chain.n
            PER_TURN = UNROLL * (2 + 2 * 3)
            with vec.Fori(1, NTURN - 1) as r:
                ring = Ring(r * TURN + (FIRST - TURN), FIRST % 2)
                chain = Chain(vec, dve, r * PER_TURN + (base - PER_TURN))
                for u in range(UNROLL):
                    head(r * UNROLL + u, u, ring, chain)
                assert chain.n == PER_TURN
            ring = Ring(FIRST + (NTURN - 2) * TURN, FIRST % 2)
            chain = Chain(vec, dve, base + (NTURN - 2) * PER_TURN)
            for u in range(UNROLL):
                head(NHEAD - UNROLL + u, u, ring, chain, last=True)
            low(NHEAD - 1, STEPS - 1)
            output(NHEAD - 1, 1, *ring.next(), chain)


def mix(nc, x, w_proj, w_q, ident_in, ao, x2_d, xn_d, q_d, mvq):
    with ExitStack() as ctx:
        sb, psum, sem = allocators(nc, ctx, "mx")
        NCH = TQ // CH
        TT = NCH * TPC
        ident = sb("ident", [P, P])
        wp = sb("wp", [P, DC, D])
        wq = sb("wq", [P, DC, QC * P])
        xt = sb("xt", [P, TT, D])
        at = [sb(f"at{u}", [P, D]) for u in range(2)]
        att = [sb(f"att{u}", [P, D]) for u in range(2)]
        x2 = [sb(f"x2{u}", [P, D]) for u in range(2)]
        xn = [sb(f"xn{u}", [P, D]) for u in range(2)]
        xnt = [sb(f"xnt{u}", [P, DC, CH]) for u in range(2)]
        qs = [sb(f"qs{u}", [P, TPC, 4, P]) for u in range(4)]
        st = sb("st", [P, 6])
        mv = sb("mv", [P, 2])
        sd = sb("sd", [P, 1])
        rstd = sb("rstd", [P, 1])
        nmr = sb("nmr", [P, 1])
        eps = sb("eps", [P, 1])
        stq = sb("stq", [P, QC, NCH * B, 6])
        tp = [psum(f"tp{u}", [P, CH]) for u in range(2)]
        yp = [psum(f"yp{u}", [P, CH]) for u in range(2)]
        qp = [psum(f"qp{u}", [P, CH]) for u in range(4)]

        consts_in = sem("consts_in")
        x_in = sem("x_in")
        at_made = sem("at_made")
        at_turned = sem("at_turned")
        att_made = sem("att_made")
        y_full = sem("y_full")
        x2_made = sem("x2_made")
        stats_done = sem("stats_done")
        sd_done = sem("sd_done")
        scale_done = sem("scale_done")
        xn_made = sem("xn_made")
        xn_turned = sem("xn_turned")
        xnt_made = sem("xnt_made")
        q_full = sem("q_full")
        q_copied = sem("q_copied")
        q_counted = sem("q_counted")
        rows_out = [sem(f"rows_out{u}") for u in range(2)]
        q_out = [sem(f"q_out{u}") for u in range(4)]
        eps_done = sem("eps_done")
        passed = sem("passed")
        dve = sem("dve")
        NQ = NCH * QC

        block = ctx.enter_context(nc.Block())

        @block.sync
        def _(sp):
            sp.dma_start(ident[:], ident_in).then_inc(consts_in, 16)
            sp.dma_start(wp[:], w_proj.rearrange("(c p) e -> p c e", p=P)).then_inc(consts_in, 16)
            sp.dma_start(wq[:], w_q.rearrange("(c p) e -> p c e", p=P)).then_inc(consts_in, 16)
            x_v = x.rearrange("b (n p) d -> p (b n) d", p=P)
            with sp.Fori(0, B) as r:
                sp.wait_ge(x2_made, r * TT)
                sp.dma_start(xt[:], x_v[:, bass.ds(r * TT, TT), :]).then_inc(x_in, 16)
                def store_rows(t):
                    sp.wait_ge(xn_made, r * TT + t + 1)
                    sp.dma_start(x2_d[bass.ds(r * TQ + t * P, P), :], x2[t % 2][:]).then_inc(rows_out[t % 2], 16)
                    sp.dma_start(xn_d[bass.ds(r * TQ + t * P, P), :], xn[t % 2][:]).then_inc(rows_out[t % 2], 16)

                for t in range(TPC):
                    store_rows(t)
                for c in range(NCH):
                    for k in range(QC // 4):
                        if c + 1 < NCH:
                            store_rows((c + 1) * TPC + k)
                        sp.wait_ge(q_copied, r * NQ + c * QC + 4 * k + 4)
                        dst = q_d[bass.ds(r * TT + c * TPC, TPC), :, 4 * k:4 * k + 4, :]
                        sp.dma_start(dst.rearrange("s p k t -> p s (k t)"),
                                     qs[k][:].rearrange("p s k t -> p s (k t)")).then_inc(q_out[k], 16)
            for u in range(2):
                sp.wait_ge(rows_out[u], 32 * NT // 2)
            for u in range(4):
                sp.wait_ge(q_out[u], 16 * B * NCH)

        @block.gpsimd
        def _(pool):
            with pool.Fori(0, B) as r:
                for t in range(TT):
                    if t >= 2:
                        pool.wait_ge(at_turned, r * TT + t - 1)
                    else:
                        pool.wait_ge(at_turned, r * TT)
                    src = ao[:, bass.ds(r * H, H), t, :]
                    pool.tensor_copy(at[t % 2][:].rearrange("p (h d) -> p h d", h=H), src).then_inc(at_made, 1)

        @block.tensor
        def _(pe):
            pe.wait_ge(consts_in, 48)
            with pe.Fori(0, B) as r:
                def turn_attended(t):
                    pe.wait_ge(at_made, r * TT + t + 1)
                    pe.wait_ge(att_made, r * TT + t)
                    for c in range(DC):
                        last = pe.transpose(tp[0][:, c * P:(c + 1) * P], at[t % 2][:, c * P:(c + 1) * P], ident[:])
                    last.then_inc(at_turned, 1)

                def output(t):
                    pe.wait_ge(att_made, r * TT + t + 1)
                    pe.wait_ge(x2_made, r * TT + max(t - 1, 0))
                    for c in range(DC):
                        last = pe.matmul(yp[t % 2][:], att[t % 2][:, c * P:(c + 1) * P], wp[:, c, :],
                                         start=(c == 0), stop=(c == DC - 1))
                    last.then_inc(y_full, 1)

                def turn_normed(t):
                    pe.wait_ge(xn_made, r * TT + t + 1)
                    pe.wait_ge(xnt_made, r * TT + t)
                    for c in range(DC):
                        last = pe.transpose(tp[1][:, c * P:(c + 1) * P], xn[t % 2][:, c * P:(c + 1) * P], ident[:])
                    last.then_inc(xn_turned, 1)

                def queries(c, k):
                    n = c * QC + k
                    if k == 0:
                        pe.wait_ge(xnt_made, r * TT + (c + 1) * TPC)
                    if n >= 4:
                        pe.wait_ge(q_copied, r * NQ + n - 3)
                    else:
                        pe.wait_ge(q_copied, r * NQ)
                    for d in range(DC):
                        last = pe.matmul(qp[n % 4][:], wq[:, d, k * P:(k + 1) * P], xnt[c % 2][:, d, :],
                                         start=(d == 0), stop=(d == DC - 1))
                    last.then_inc(q_full, 1)

                def front(c, part):
                    t = c * TPC + part // 3
                    (turn_attended, output, turn_normed)[part % 3](t)

                for part in range(3 * TPC):
                    front(0, part)
                for k in range(QC):
                    queries(0, k)
                    if k < 3 * TPC:
                        front(1, k)
                for k in range(QC):
                    queries(1, k)

        @block.scalar
        def _(act):
            act.wait_ge(eps_done, 1)
            with act.Fori(0, B) as r:
                def copy_attended(t):
                    act.wait_ge(at_turned, r * TT + t + 1)
                    act.wait_ge(y_full, r * TT + max(t - 1, 0))
                    act.activation(att[t % 2][:], tp[0][:], ACT.Copy).then_inc(att_made, 1)

                def spread(t):
                    act.wait_ge(stats_done, r * TT + t + 1)
                    act.activation(sd[:], mv[:, 1:2], ACT.Sqrt, bias=eps[:]).then_inc(sd_done, 1)

                def copy_normed(t):
                    act.wait_ge(xn_turned, r * TT + t + 1)
                    c, s = divmod(t, TPC)
                    if s == 0:
                        act.wait_ge(q_full, r * NQ + max(c - 1, 0) * QC)
                    act.activation(xnt[c % 2][:, :, s * P:(s + 1) * P],
                                   tp[1][:].rearrange("p (c t) -> p c t", c=DC), ACT.Copy).then_inc(xnt_made, 1)

                def query(c, k):
                    n = c * QC + k
                    act.wait_ge(q_full, r * NQ + n + 1)
                    act.wait_ge(q_out[k // 4], r * (16 * NCH) + 16 * c)
                    act.wait_ge(q_counted, r * NQ + c * QC)
                    act.activation(qs[k // 4][:, :, k % 4, :], qp[n % 4][:].rearrange("p (s t) -> p s t", s=TPC),
                                   ACT.Copy).then_inc(q_copied, 1)

                def front(c, part):
                    t = c * TPC + part // 3
                    (copy_attended, spread, copy_normed)[part % 3](t)

                for part in range(3 * TPC):
                    front(0, part)
                for k in range(QC):
                    query(0, k)
                    if k < 3 * TPC:
                        front(1, k)
                for k in range(QC):
                    query(1, k)

        @block.vector
        def _(vec):
            vec.memset(eps[:], EPS).then_inc(eps_done, 1)
            LINKS = 2
            with vec.Fori(0, B) as r:
                chain = Chain(vec, dve, r * (LINKS * TT))
                vec.wait_ge(x_in, r * 16 + 16)

                def front(t):
                    vec.wait_ge(y_full, r * TT + t + 1)
                    vec.wait_ge(rows_out[t % 2], r * (16 * TT) + 32 * (t // 2))
                    vec.wait_ge(xn_turned, r * TT + max(t - 1, 0))
                    vec.tensor_tensor(x2[t % 2][:], yp[t % 2][:], xt[:, t, :], ALU.add).then_inc(x2_made, 1)
                    vec.wait_ge(x2_made, r * TT + t + 1)
                    chain.link(vec.bn_stats(st[:], x2[t % 2][:]))
                    gate(vec, passed)
                    vec.bn_aggr(mv[:], st[:]).then_inc(stats_done, 1)
                    vec.wait_ge(sd_done, r * TT + t + 1)
                    chain.link(vec.reciprocal(rstd[:], sd[:]))
                    vec.scalar_tensor_tensor(out=nmr[:], in0=mv[:, 0:1], scalar=-1.0, in1=rstd[:],
                                             op0=ALU.mult, op1=ALU.mult).then_inc(scale_done, 1)
                    vec.wait_ge(scale_done, r * TT + t + 1)
                    vec.tensor_scalar(xn[t % 2][:], x2[t % 2][:], rstd[:], nmr[:], ALU.mult,
                                      ALU.add).then_inc(xn_made, 1)

                def query(c, k):
                    vec.wait_ge(q_copied, r * NQ + c * QC + k + 1)
                    g = r * NCH + c
                    vec.bn_stats(stq[:, k, bass.ds(g, 1), :].rearrange("p o s -> p (o s)"),
                                 qs[k // 4][:, :, k % 4, :]).then_inc(q_counted, 1)

                for t in range(TPC):
                    front(t)
                for k in range(QC):
                    query(0, k)
                    if k < 3 * TPC and k % 3 == 1:
                        front(TPC + k // 3)
                for k in range(QC):
                    query(1, k)
            vec.wait_ge(q_counted, B * NQ)
            for k in range(QC):
                vec.bn_aggr(mvq[:, k, :], stq[:, k, :, :].rearrange("p g s -> p (g s)"))


def experts(nc, table, keys_t, gamma_t, beta_t, ident_in, mvq, x2_d, xn_d, q_d, out):
    with ExitStack() as ctx:
        sb, psum, sem = allocators(nc, ctx, "ex")
        RG = 4
        ident = sb("ident", [P, P])
        keys = sb("keys", [P, QC, NKEY])
        gam = sb("gam", [P, QC])
        bet = sb("bet", [P, QC])
        eps = sb("eps", [P, 1])
        qsc = sb("qsc", [P, QC])
        qbi = sb("qbi", [P, QC])
        qt = sb("qt", [P, QC, P])
        qn = sb("qn", [P, QC, P])
        xn = [sb(f"xn{u}", [P, D]) for u in range(2)]
        x2 = [sb(f"x2{u}", [P, D]) for u in range(2)]
        yo = sb("yo", [P, D])
        ring = [sb(f"ring{g}", [P, TOPK, EW]) for g in range(RG)]
        diag = [sb(f"diag{k}", [P, P]) for k in range(TOPK)]
        eight_i = sb("eight_i", [P, TOPK], I32)
        eight = sb("eight", [P, TOPK])
        top = sb("top", [P, QC, TOPK])
        pos = sb("pos", [P, QC, TOPK], U32)
        posf = sb("posf", [P, QC, TOPK])
        cand = sb("cand", [P, PH, TOPK * TOPK])
        best = sb("best", [P, PH, TOPK])
        pick = sb("pick", [P, 2, NSLOT], U32)
        pickf = sb("pickf", [P, 2, NSLOT])
        hot = sb("hot", [P, NSLOT, TOPK])
        sel = sb("sel", [P, 2, NSLOT])
        idx = [sb(f"idx{u}", [P, NSLOT], U32) for u in range(2)]
        shifted = sb("shifted", [P, PH, TOPK])
        expd = sb("expd", [P, PH, TOPK])
        esum = sb("esum", [P, PH])
        wgt = [sb(f"wgt{u}", [P, PH, TOPK]) for u in range(2)]
        hid = sb("hid", [P, TOPK])
        g1 = sb("g1", [P, TOPK])
        g2 = sb("g2", [P, TOPK])
        g3 = sb("g3", [P, TOPK])
        g4 = sb("g4", [P, TOPK])
        wh = sb("wh", [P, TOPK])
        coef = sb("coef", [P, TOPK])
        sim = [psum(f"sim{u}", [P, 4, NKEY]) for u in range(4)]
        acc = [psum(f"acc{u}", [P, D]) for u in range(2)]

        consts_in = sem("consts_in")
        q_in = sem("q_in")
        x_in = [sem(f"x_in{u}") for u in range(2)]
        qn_made = sem("qn_made")
        sim_made = sem("sim_made")
        sim_read = sem("sim_read")
        shift_made = sem("shift_made")
        exp_made = sem("exp_made")
        routed = sem("routed")
        rows_in = [sem(f"rows_in{g}") for g in range(RG)]
        arg_made = sem("arg_made")
        gelu_exp = sem("gelu_exp")
        coef_made = sem("coef_made")
        diag_made = sem("diag_made")
        diag_used = sem("diag_used")
        y_made = sem("y_made")
        y_out = sem("y_out")
        qsd_made = sem("qsd_made")
        aff_made = sem("aff_made")
        eight_made = sem("eight_made")
        passed = sem("passed")
        mv_ready = sem("mv_ready")
        dve = sem("dve")

        ROUTE_LINKS = 17
        GROUP_LINKS = TOPK + 6
        TILE_LINKS = ROUTE_LINKS + PH * GROUP_LINKS

        block = ctx.enter_context(nc.Block())

        @block.sync
        def _(sp):
            sp.dma_start(ident[:], ident_in).then_inc(consts_in, 16)
            sp.dma_start(keys[:], keys_t).then_inc(consts_in, 16)
            sp.dma_start(gam[:], gamma_t).then_inc(consts_in, 16)
            sp.dma_start(bet[:], beta_t).then_inc(consts_in, 16)

            def load(t, u):
                sp.dma_start(qt[:].rearrange("p c t -> p (c t)"),
                             q_d[bass.ds(t, 1), :, :, :].rearrange("o p c t -> (o p) (c t)")).then_inc(q_in, 16)
                sp.dma_start(xn[u][:], xn_d[bass.ds(t * P, P), :]).then_inc(x_in[u], 16)
                sp.dma_start(x2[u][:], x2_d[bass.ds(t * P, P), :]).then_inc(x_in[u], 16)

            def tile(t, u):
                sp.wait_ge(qn_made, t * QC + QC)
                if u == 1:
                    sp.wait_ge(y_made, t)
                else:
                    sp.wait_ge(y_made, t)
                load(t + 1, 1 - u)

            def store(t):
                sp.wait_ge(y_made, t + 1)
                sp.dma_start(out[bass.ds(t * P, P), :], yo[:]).then_inc(y_out, 16)

            load(0, 0)
            with sp.Fori(0, NT // 2 - 1) as r:
                for u in range(2):
                    tile(r * 2 + u, u)
                    store(r * 2 + u)
            tile(NT - 2, 0)
            store(NT - 2)
            store(NT - 1)
            sp.wait_ge(y_out, 16 * NT)

        @block.gpsimd
        def _(pool):
            pool.iota(eight_i[:], pattern=[[1, TOPK]], base=0, channel_multiplier=0).then_inc(eight_made, 1)
            with pool.Fori(0, NT // 2) as r:
                for u in range(2):
                    pool.wait_ge(routed, r * 2 + u + 1)
                    for g in range(PH):
                        pool.wait_ge(diag_used, r * (2 * PH) + u * PH + g + 1)
                        gate(pool, passed)
                        for k in range(TOPK):
                            n = g * TOPK + k
                            pool.indirect_dma_start(
                                ring[g % RG][:, k, :], None, table,
                                bass.IndirectOffsetOnAxis(ap=idx[u][:, n:n + 1], axis=0),
                            ).then_inc(rows_in[g % RG], 16)

        @block.tensor
        def _(pe):
            pe.wait_ge(consts_in, 64)

            def similar(t):
                pe.wait_ge(sim_read, t)
                for c in range(QC):
                    pe.wait_ge(qn_made, t * QC + c + 1)
                    last = pe.matmul(sim[c // 4][:, c % 4, :], qn[:, c, :], keys[:, c, :], start=True, stop=True)
                last.then_inc(sim_made, 1)

            def group(t, u, g):
                if g == 0:
                    pe.wait_ge(y_made, max(t - 1, 0) if isinstance(t, int) else t - 1)
                pe.wait_ge(rows_in[g % RG], t * (PH // RG * TOPK * 16) + (g // RG + 1) * TOPK * 16)
                for k in range(TOPK):
                    pe.wait_ge(diag_made, t * NSLOT + g * TOPK + k + 1)
                    last = pe.matmul(acc[u][:], diag[k][:], ring[g % RG][:, k, D:EW],
                                     start=(g == 0 and k == 0), stop=(g == PH - 1 and k == TOPK - 1))
                last.then_inc(diag_used, 1)

            def tile(t, u, routes=True):
                for g in range(PH):
                    if g == 3 and routes:
                        similar(t + 1)
                    group(t, u, g)

            similar(0)
            for u in range(2):
                tile(u, u)
            with pe.Fori(1, NT // 2 - 1) as r:
                for u in range(2):
                    tile(r * 2 + u, u)
            tile(NT - 2, 0)
            tile(NT - 1, 1, routes=False)

        @block.scalar
        def _(act):
            act.wait_ge(aff_made, 1)
            act.activation(qsc[:], mvq[:, :, 1], ACT.Sqrt, bias=eps[:]).then_inc(qsd_made, 1)
            act.wait_ge(aff_made, 2)

            def affine(t):
                act.wait_ge(q_in, t * 16 + 16)
                act.wait_ge(sim_made, t)
                for c in range(QC):
                    act.activation(qn[:, c, :], qt[:, c, :], ACT.Identity, bias=qbi[:, c:c + 1],
                                   scale=qsc[:, c:c + 1]).then_inc(qn_made, 1)

            def weights(t):
                act.wait_ge(shift_made, t + 1)
                act.activation(expd[:], shifted[:], ACT.Exp).then_inc(exp_made, 1)

            def group(t, g):
                n = t * PH + g
                act.wait_ge(arg_made, n + 1)
                act.activation(g4[:], g3[:], ACT.Exp).then_inc(gelu_exp, 1)
                act.wait_ge(coef_made, n + 1)
                act.wait_ge(diag_used, n + RG)
                for k in range(TOPK):
                    act.activation(diag[k][:], ident[:], ACT.Copy, scale=coef[:, k:k + 1]).then_inc(diag_made, 1)

            def tile(t, routes=True):
                for g in range(PH):
                    if g == 2 and routes:
                        affine(t + 1)
                    group(t, g)
                    if g == 3 and routes:
                        weights(t + 1)

            act.wait_ge(consts_in, 64)
            affine(0)
            weights(0)
            with act.Fori(0, NT - 1) as t:
                tile(t)
            tile(NT - 1, routes=False)

        @block.vector
        def _(vec):
            chain = Chain(vec, dve)
            vec.nop().then_inc(diag_used, RG)
            chain.mark(vec.memset(eps[:], EPS))
            chain.settle()
            vec.nop().then_inc(aff_made, 1)
            vec.wait_ge(eight_made, 1)
            vec.wait_ge(consts_in, 64)
            chain.mark(vec.tensor_copy(eight[:], eight_i[:]))
            vec.wait_ge(qsd_made, 1)
            chain.link(vec.reciprocal(qbi[:], qsc[:]))
            chain.link(vec.tensor_tensor(qsc[:], qbi[:], gam[:], ALU.mult))
            chain.link(vec.tensor_tensor(qbi[:], mvq[:, :, 0], qsc[:], ALU.mult))
            vec.tensor_tensor(qbi[:], bet[:], qbi[:], ALU.subtract).then_inc(aff_made, 1)

            def route(t, u, chain):
                start = chain.n
                vec.wait_ge(sim_made, t + 1)
                gate(vec, passed)
                for c in range(QC):
                    last = vec.max(top[:, c, :], sim[c // 4][:, c % 4, :])
                chain.link(last)
                gate(vec, passed)
                for c in range(QC):
                    last = vec.max_index(pos[:, c, :], top[:, c, :], sim[c // 4][:, c % 4, :])
                last.then_inc(sim_read, 1)
                vec.wait_ge(sim_read, t + 1)
                chain.mark(vec.tensor_copy(posf[:], pos[:]))
                pair = [P, PH, TOPK, TOPK]
                chain.link(vec.tensor_tensor(cand[:].rearrange("p h (a b) -> p h a b", a=TOPK),
                                             top[:, 0:PH, :].unsqueeze(3).to_broadcast(pair),
                                             top[:, PH:QC, :].unsqueeze(2).to_broadcast(pair), ALU.add))
                gate(vec, passed)
                for h in range(PH):
                    last = vec.max(best[:, h, :], cand[:, h, :])
                chain.link(last)
                gate(vec, passed)
                for h in range(PH):
                    last = vec.max_index(pick[:, 0, h * TOPK:(h + 1) * TOPK], best[:, h, :], cand[:, h, :])
                chain.link(last)
                vec.tensor_tensor(shifted[:], best[:], best[:, :, 0:1].to_broadcast([P, PH, TOPK]),
                                  ALU.subtract).then_inc(shift_made, 1)
                chain.link(vec.tensor_scalar(pick[:, 1, :], pick[:, 0, :], 7, None, ALU.bitwise_and))
                chain.link(vec.tensor_scalar(pick[:, 0, :], pick[:, 0, :], 3, None, ALU.logical_shift_right))
                chain.link(vec.tensor_copy(pickf[:], pick[:]))
                for side in range(2):
                    chain.link(vec.tensor_tensor(
                        hot[:], pickf[:, side, :].unsqueeze(2).to_broadcast([P, NSLOT, TOPK]),
                        eight[:].unsqueeze(1).to_broadcast([P, NSLOT, TOPK]), ALU.is_equal))
                    hot4 = hot[:].rearrange("p (h k) a -> p h k a", h=PH)
                    chain.link(vec.tensor_tensor(
                        hot4, hot4, posf[:, side * PH:(side + 1) * PH, :].unsqueeze(2).to_broadcast(pair), ALU.mult))
                    chain.link(vec.tensor_reduce(sel[:, side, :], hot[:], AX.X, ALU.add))
                vec.scalar_tensor_tensor(out=idx[u][:], in0=sel[:, 0, :], scalar=float(NKEY), in1=sel[:, 1, :],
                                         op0=ALU.mult, op1=ALU.add).then_inc(routed, 1)
                vec.wait_ge(exp_made, t + 1)
                chain.link(vec.tensor_reduce(esum[:], expd[:], AX.X, ALU.add))
                chain.link(vec.reciprocal(esum[:], esum[:]))
                chain.mark(vec.tensor_tensor(wgt[u][:], expd[:], esum[:].unsqueeze(2).to_broadcast([P, PH, TOPK]),
                                             ALU.mult))
                assert chain.n == start + ROUTE_LINKS

            def group(t, u, g, chain):
                start = chain.n
                if g == 0:
                    vec.wait_ge(x_in[u], (t // 2) * 32 + 32)
                vec.wait_ge(rows_in[g % RG], t * (PH // RG * TOPK * 16) + (g // RG + 1) * TOPK * 16)
                for k in range(TOPK):
                    down = ring[g % RG][:, k, 0:D]
                    chain.mark(vec.tensor_tensor_reduce(down, down, xn[u][:], 1.0, 0.0,
                                                        ALU.mult, ALU.add, hid[:, k:k + 1]))
                chain.settle()
                chain.link(vec.tensor_tensor(g1[:], hid[:], hid[:], ALU.mult))
                chain.link(vec.tensor_scalar(g2[:], g1[:], -2 * GELU_C * 0.044715, -2 * GELU_C, ALU.mult, ALU.add))
                chain.link(vec.tensor_tensor(g1[:], g2[:], hid[:], ALU.mult))
                vec.tensor_scalar(g3[:], g1[:], 80.0, None, ALU.min).then_inc(arg_made, 1)
                chain.link(vec.tensor_tensor(wh[:], hid[:], wgt[u][:, g, :], ALU.mult))
                vec.wait_ge(gelu_exp, t * PH + g + 1)
                chain.link(vec.tensor_scalar(g2[:], g4[:], 1.0, None, ALU.add))
                chain.link(vec.reciprocal(g2[:], g2[:]))
                vec.wait_ge(diag_made, t * NSLOT + g * TOPK)
                vec.tensor_tensor(coef[:], wh[:], g2[:], ALU.mult).then_inc(coef_made, 1)
                assert chain.n == start + GROUP_LINKS

            def finish(t, u):
                vec.wait_ge(diag_used, t * PH + PH + RG)
                vec.wait_ge(y_out, t * 16)
                vec.tensor_tensor(yo[:], acc[u][:], x2[u][:], ALU.add).then_inc(y_made, 1)

            def tile(t, u, chain, routes=True):
                for g in range(PH):
                    group(t, u, g, chain)
                    if g == 3 and routes:
                        route(t + 1, 1 - u, chain)
                finish(t, u)

            route(0, 0, chain)
            base = chain.n
            with vec.Fori(0, NT // 2 - 1) as r:
                chain = Chain(vec, dve, r * (2 * TILE_LINKS) + base)
                for u in range(2):
                    tile(r * 2 + u, u, chain)
            chain = Chain(vec, dve, (NT - 2) * TILE_LINKS + base)
            tile(NT - 2, 0, chain)
            tile(NT - 1, 1, chain, routes=False)


def program(nc, x, ctx_t, w_q, w_kv, w_proj, w_rel, f_wq, gamma_t, beta_t, keys_t, table, ident, out):
    with ExitStack() as ctx:
        def dram(name, shape):
            return nc.dram_tensor(name, shape, F32, kind="Internal").ap()

        qa_d = dram("qa_d", [2, NHEAD * DH, TQ])
        ka_d = dram("ka_d", [2, NHEAD * DH, TK])
        bq_d = dram("bq_d", [H, 4, TQ])
        m_d = dram("m_d", [4, 2, TQ])
        x2_d = dram("x2_d", [B * TQ, D])
        xn_d = dram("xn_d", [B * TQ, D])
        q_d = dram("q_d", [NT, P, QC, P])
        mvq = ctx.enter_context(nc.sbuf_tensor("mvq", [P, QC, 2], F32))
        with ExitStack() as attention:
            ao = attention.enter_context(nc.sbuf_tensor("ao", [P, NHEAD, QT, DH], F32))
            with ExitStack() as values:
                v_all = values.enter_context(nc.sbuf_tensor("v_all", [P, NHEAD, KT, DH], F32))
                project(nc, x, ctx_t, w_q, w_kv, w_rel, ident, qa_d, ka_d, bq_d, v_all)
                attend(nc, qa_d, ka_d, bq_d, m_d, v_all, ao, ident)
            mix(nc, x, w_proj, f_wq, ident, ao, x2_d, xn_d, q_d, mvq)
        experts(nc, table, keys_t, gamma_t, beta_t, ident, mvq, x2_d, xn_d, q_d, out)


def kernel(**inputs):
    import numpy as np
    import concourse.bacc as bacc
    from concourse.bass_utils import run_bass_kernel_spmd

    a = {k: np.asarray(v) for k, v in inputs.items()}
    c = np.ascontiguousarray
    arrays = {
        "x": a["x"],
        "ctx_t": c(a["ctx_1024"].reshape(B * TK, D).T),
        "w_q": a["L0_xattn_w_q"],
        "w_kv": a["L0_xattn_w_kv"],
        "w_proj": a["L0_xattn_w_proj"],
        "w_rel": a["L0_xattn_w_rel"],
        "f_wq": a["L0_ffn_w_q"],
        "gamma_t": c(a["L0_ffn_bn_gamma"].reshape(QC, P).T),
        "beta_t": c(a["L0_ffn_bn_beta"].reshape(QC, P).T),
        "keys_t": c(a["L0_ffn_keys"].transpose(3, 2, 0, 1).reshape(KD, QC, NKEY)),
        "table": np.concatenate([a["L0_ffn_down_embed"], a["L0_ffn_up_embed"]], axis=1),
        "ident": np.eye(P, dtype=np.float32),
    }
    nc = bacc.Bacc("TRN2", target_bir_lowering=False, num_devices=1)
    aps = [nc.dram_tensor(n, v.shape, mybir.dt.from_np(v.dtype), kind="ExternalInput").ap() for n, v in arrays.items()]
    out = nc.dram_tensor("out", [B * TQ, D], F32, kind="ExternalOutput").ap()
    program(nc, *aps, out)
    r = run_bass_kernel_spmd(nc, [arrays], core_ids=[0])
    return r.results[0]["out"].reshape(B, TQ, D)
```

```python
from contextlib import ExitStack

import concourse.bass as bass
from concourse import mybir

F32 = mybir.dt.float32
F32R = mybir.dt.float32r
U32 = mybir.dt.uint32
I32 = mybir.dt.int32
ALU = mybir.AluOpType
ACT = mybir.ActivationFunctionType
AX = mybir.AxisListType

P = 128
B, TQ, TK, D = 2, 1024, 2048, 512
H, DH = 16, 32
SCALE = DH ** -0.5
EPS = 1e-5
NHEAD = B * H
DC = D // P
CH = 512
TPC = CH // P
NT = B * TQ // P
QT = TQ // P
KT = TK // P
PH, KD, NKEY, TOPK = 8, 128, 128, 8
QC = 2 * PH
EW = 2 * D
NSLOT = PH * TOPK
GELU_C = (2.0 / 3.141592653589793) ** 0.5

BIAS0 = 3 * DH
MAX0 = BIAS0 + 4
KROWS = MAX0 + 2


def allocators(nc, ctx, tag):
    def sb(name, shape, dt=F32):
        return ctx.enter_context(nc.sbuf_tensor(f"{tag}_{name}", shape, dt))

    def psum(name, shape):
        return ctx.enter_context(nc.psum_tensor(f"{tag}_{name}", shape, F32))

    def sem(name):
        return ctx.enter_context(nc.semaphore(f"{tag}_{name}"))

    return sb, psum, sem


def gate(eng, passed):
    eng.sem_inc(passed, 1)


def wait_count(eng, sem, count):
    if not isinstance(count, int) or count > 0:
        eng.wait_ge(sem, count)


class Chain:

    def __init__(self, eng, sem, base=0):
        self.eng, self.sem, self.base, self.n = eng, sem, base, 0

    def mark(self, ins):
        ins.then_inc(self.sem, 1)
        self.n += 1

    def settle(self):
        self.eng.wait_ge(self.sem, self.base + self.n)

    def link(self, ins):
        self.mark(ins)
        self.settle()


def project(nc, x, ctx_t, w_q, w_kv, w_rel, ident_in, qa_d, ka_d, bq_d, kc_d, v_all, ao):
    with ExitStack() as ctx:
        sb, psum, sem = allocators(nc, ctx, "pj")
        NTURN = B * TQ // CH
        OUTB = 2
        BLOCKS = TQ // P
        ident = sb("ident", [P, P])
        K, V, Q = range(3)
        w_hi = [sb(f"w_hi{g}", [P, DC, D]) for g in range(3)]
        w_lo = [sb(f"w_lo{g}", [P, DC, D]) for g in range(3)]
        ct_hi = [sb(f"ct_hi{u}", [P, DC, CH]) for u in range(2)]
        ct_lo = [sb(f"ct_lo{u}", [P, DC, CH]) for u in range(2)]
        xt_hi = sb("xt_hi", [P, DC, CH])
        xt_lo = sb("xt_lo", [P, DC, CH])
        hi = [sb(f"hi{u}", [P, CH]) for u in range(OUTB)]
        lo = [sb(f"lo{u}", [P, CH]) for u in range(OUTB)]
        stats = sb("stats", [P, TPC, 6])
        mv = sb("mv", [P, TPC, 2])
        sd = sb("sd", [P, TPC])
        rstd = sb("rstd", [P, TPC])
        nmr = sb("nmr", [P, TPC])
        eps = sb("eps", [P, 1])
        wr = sb("wr", [P, 1])
        ii = sb("ii", [P, P], I32)
        iw = sb("iw", [P, P])
        bq = sb("bq", [P, 4, P])
        nj_int = sb("nj_int", [KT, P], I32)
        kc = sb("kc", [KT, KROWS - BIAS0, P])
        acc = [psum(f"acc{u}", [P, CH]) for u in range(4)]
        tp = [psum(f"tp{u}", [P, CH]) for u in range(2)]

        ROOM = NHEAD // 4
        raw = [ao[:, i * ROOM:(i + 1) * ROOM, :, :].rearrange("p n q d -> p (n q d)").rearrange(
            "p (c t) -> p c t", c=DC) for i in range(4)]
        raw_ct, xt, xn = raw[0:2], raw[2], raw[3]
        raw_w = [v_all[:, H + g * H // 4:H + (g + 1) * H // 4, :, :].rearrange("p n k d -> p (n k d)").rearrange(
            "p (c t) -> p c t", c=DC) for g in range(3)]

        ident_here = sem("ident_here")
        wr_in = sem("wr_in")
        w_in = [sem(f"w_in{g}") for g in range(3)]
        w_hi_made = sem("w_hi_made")
        w_lo_made = sem("w_lo_made")
        x_in = sem("x_in")
        ct_in = [sem(f"ct_in{u}") for u in range(2)]
        ct_hi_made = sem("ct_hi_made")
        ct_lo_made = sem("ct_lo_made")
        acc_full = sem("acc_full")
        acc_free = sem("acc_free")
        hi_done = sem("hi_done")
        out_done = [sem(f"out_done{u}") for u in range(OUTB)]
        stats_done = sem("stats_done")
        sd_done = sem("sd_done")
        dve = sem("dve")
        scale_done = sem("scale_done")
        xn_done = sem("xn_done")
        tp_full = sem("tp_full")
        xt_hi_made = sem("xt_hi_made")
        xt_lo_made = sem("xt_lo_made")
        iota_done = sem("iota_done")
        bias_done = sem("bias_done")
        bias_out = sem("bias_out")
        eps_done = sem("eps_done")
        passed = sem("passed")

        plan = []
        for u in range(2):
            plan += [(K, u, e) for e in range(DC)] + [(V, u, s) for s in range(TPC)]
        plan += [(Q, 0, e) for e in range(DC)]
        NPLAN = len(plan)
        split_at = [n for n, (kind, _, _) in enumerate(plan) if kind != V]
        NSPLIT = len(split_at)
        SPLIT_CT = (2 * TPC, 4 * TPC)
        STATS_AT, SPREAD_AT, NORM_AT, TURN_AT = 2, 4, 6, 10
        SPLIT_V, SPLIT_Q = 0, 8

        def turns(eng, turn, after_first=None):
            turn(0, False)
            if after_first:
                after_first()
            with eng.Fori(1, NTURN - 1) as r:
                turn(r, False)
            turn(NTURN - 1, True)

        block = ctx.enter_context(nc.Block())

        @block.sync
        def _(sp):
            ctx_v = ctx_t.rearrange("(c p) t -> p c t", p=P)
            x_v = x.rearrange("b (n p) d -> p (b n) d", p=P)
            w_kv_v = w_kv.rearrange("(c p) e -> p c e", p=P)

            def load_ct(r, u):
                wait_count(sp, ct_lo_made, r * 2 + u - 1)
                sp.dma_start(raw_ct[u], ctx_v[:, :, bass.ds(r * (2 * CH) + u * CH, CH)]).then_inc(ct_in[u], 16)

            def load_x(r):
                wait_count(sp, xn_done, r * TPC)
                sp.dma_start(xt, x_v[:, bass.ds(r * TPC, TPC), :]).then_inc(x_in, 16)

            def turn(r, last):
                for k, n in enumerate(split_at):
                    if k < 2 and not last:
                        load_ct(r + 1, k)
                    if k == DC + 1 and not last:
                        load_x(r + 1)
                    kind, u, e = plan[n]
                    sp.wait_ge(acc_free, r * NPLAN + n + 1)
                    dst, half = (ka_d, 2 * CH) if kind == K else (qa_d, CH)
                    rows = bass.ds((r // 2) * D + e * P, P)
                    cols = bass.ds((r & 1) * half + u * CH, CH)
                    sp.dma_start(dst[0, rows, cols], hi[k % OUTB][:]).then_inc(out_done[k % OUTB], 16)
                    sp.dma_start(dst[1, rows, cols], lo[k % OUTB][:]).then_inc(out_done[k % OUTB], 16)

            def store_bias():
                sp.wait_ge(bias_done, 2)
                sp.dma_start(bq_d.rearrange("r h (b t) -> (h b) r t", t=P), bq[:]).then_inc(bias_out, 16)
                sp.dma_start(kc_d.rearrange("r (b t) -> b r t", t=P), kc[:]).then_inc(bias_out, 16)

            sp.dma_start(raw_w[K], w_kv_v[:, :, 0:D]).then_inc(w_in[K], 16)
            load_ct(0, 0)
            sp.dma_start(raw_w[V], w_kv_v[:, :, D:2 * D]).then_inc(w_in[V], 16)
            load_ct(0, 1)
            load_x(0)
            sp.dma_start(raw_w[Q], w_q.rearrange("(c p) e -> p c e", p=P)).then_inc(w_in[Q], 16)
            sp.dma_start(ident[:], ident_in).then_inc(ident_here, 16)
            for b in range(BLOCKS):
                sp.dma_start(wr[b:P:BLOCKS, :], w_rel.rearrange("o h -> h o")).then_inc(wr_in, 16)
            turns(sp, turn, store_bias)
            sp.wait_ge(bias_out, 32)
            for u in range(OUTB):
                sp.wait_ge(out_done[u], 32 * NTURN * NSPLIT // OUTB)

        @block.gpsimd
        def _(pool):
            def split_ct(r, u):
                pool.wait_ge(ct_hi_made, r * 2 + u + 1)
                pool.tensor_tensor(ct_lo[u][:].bitcast(F32R), raw_ct[u], ct_hi[u][:], ALU.subtract).then_inc(ct_lo_made, 1)

            def turn(r, last):
                if not last:
                    for u in range(2):
                        split_ct(r + 1, u)

            pool.wait_ge(ct_lo_made, 1)
            split_ct(0, 1)
            pool.iota(ii[:], pattern=[[1, P]], base=0, channel_multiplier=P).then_inc(iota_done, 1)
            pool.iota(nj_int[:], pattern=[[-1, P]], base=0, channel_multiplier=-P).then_inc(iota_done, 1)
            turns(pool, turn)

        @block.tensor
        def _(pe):
            def turn_tokens(r, c):
                pe.wait_ge(xn_done, r * TPC + TPC)
                pe.wait_ge(ident_here, 16)
                wait_count(pe, xt_lo_made, r * DC + c - 1)
                for s in range(TPC):
                    last = pe.transpose(tp[c % 2][:, s * P:(s + 1) * P], xn[:, s, c * P:(c + 1) * P], ident[:])
                last.then_inc(tp_full, 1)

            def product(r, n):
                kind, u, part = plan[n]
                if part == 0 and u == 0:
                    wait_count(pe, w_lo_made, kind + 1 if isinstance(r, int) and r == 0 else 0)
                if kind == Q and part == 0:
                    pe.wait_ge(xt_lo_made, r * DC + DC)
                if kind == K and part == 0:
                    pe.wait_ge(ct_lo_made, r * 2 + u + 1)
                if kind == Q:
                    token_hi, token_lo = xt_hi, xt_lo
                else:
                    token_hi, token_lo = ct_hi[u], ct_lo[u]
                wait_count(pe, acc_free, r * NPLAN + n - 3)
                piece = slice(part * P, (part + 1) * P)
                for c in range(DC):
                    for k in range(3):
                        if kind == V:
                            weight = (w_lo if k == 1 else w_hi)[kind]
                            token = token_lo if k == 2 else token_hi
                            lhs, rhs = token[:, c, piece], weight[:, c, :]
                        else:
                            weight = (w_lo if k == 2 else w_hi)[kind]
                            token = token_lo if k == 1 else token_hi
                            lhs, rhs = weight[:, c, piece], token[:, c, :]
                        last = pe.matmul(acc[n % 4][:], lhs.bitcast(F32R), rhs.bitcast(F32R),
                                         start=(c == 0 and k == 0), stop=(c == DC - 1 and k == 2))
                last.then_inc(acc_full, 1)

            def turn(r, last):
                for n in range(NPLAN):
                    product(r, n)
                    if TURN_AT <= n < TURN_AT + DC:
                        turn_tokens(r, n - TURN_AT)

            turns(pe, turn)

        @block.scalar
        def _(act):
            def split_weights(g):
                act.wait_ge(w_in[g], 16)
                act.activation(w_hi[g][:].bitcast(F32R), raw_w[g], ACT.Copy).then_inc(w_hi_made, 1)

            def split_ct(r, u):
                act.wait_ge(ct_in[u], r * 16 + 16)
                wait_count(act, acc_full, (r - 1) * NPLAN + SPLIT_CT[u])
                act.activation(ct_hi[u][:].bitcast(F32R), raw_ct[u], ACT.Copy).then_inc(ct_hi_made, 1)

            def turn(r, last):
                first = isinstance(r, int) and r == 0
                for n, (kind, u, part) in enumerate(plan):
                    if kind != V:
                        k = split_at.index(n)
                        act.wait_ge(acc_full, r * NPLAN + n + 1)
                        wait_count(act, out_done[k % OUTB], r * (32 * NSPLIT // OUTB) + 32 * (k // OUTB))
                        act.activation(hi[k % OUTB][:].bitcast(F32R), acc[n % 4][:], ACT.Copy,
                                       scale=(SCALE if kind == Q else 1.0)).then_inc(hi_done, 1)
                    if n == SPREAD_AT:
                        act.wait_ge(stats_done, r + 1)
                        act.activation(sd[:], mv[:, :, 1], ACT.Sqrt, bias=eps[:]).then_inc(sd_done, 1)
                    if n == NORM_AT:
                        act.wait_ge(scale_done, r + 1)
                        for s in range(TPC):
                            act.activation(xn[:, s, :], xt[:, s, :], ACT.Identity, bias=nmr[:, s:s + 1],
                                           scale=rstd[:, s:s + 1]).then_inc(xn_done, 1)
                    if TURN_AT <= n < TURN_AT + DC:
                        c = n - TURN_AT
                        act.wait_ge(tp_full, r * DC + c + 1)
                        if c == 0:
                            wait_count(act, acc_full, r * NPLAN)
                        act.activation(xt_hi[:, c, :].bitcast(F32R), tp[c % 2][:], ACT.Copy).then_inc(xt_hi_made, 1)
                    if n in SPLIT_CT and not last:
                        split_ct(r + 1, SPLIT_CT.index(n))
                    if n == SPLIT_Q and first:
                        split_weights(Q)

            split_weights(K)
            split_ct(0, 0)
            split_weights(V)
            split_ct(0, 1)
            act.wait_ge(eps_done, 1)
            turns(act, turn)

        @block.vector
        def _(vec):
            LINKS = 2
            bias_links = 9

            def split_weights(g):
                vec.wait_ge(w_hi_made, g + 1)
                vec.tensor_tensor(w_lo[g][:].bitcast(F32R), raw_w[g], w_hi[g][:], ALU.subtract).then_inc(w_lo_made, 1)

            def bias_rows():
                chain = Chain(vec, dve, LINKS)
                chain.mark(vec.memset(kc[:], 1.0))
                vec.wait_ge(iota_done, 2)
                vec.wait_ge(wr_in, 16 * BLOCKS)
                chain.link(vec.tensor_scalar(ii[:], ii[:], TQ - 1, None, ALU.bitwise_and))
                for k in range(2):
                    last = vec.tensor_copy(kc[:, 2 + k, :].bitcast(F32R), nj_int[:])
                last.then_inc(bias_done, 1)
                chain.link(vec.tensor_copy(iw[:], ii[:]))
                chain.link(vec.tensor_scalar(iw[:], iw[:], wr[:, 0:1], None, ALU.mult))
                for k in range(2):
                    chain.link(vec.tensor_copy(bq[:, 2 * k, :].bitcast(F32R), iw[:]))
                    chain.link(vec.tensor_tensor(bq[:, 2 * k + 1, :].bitcast(F32R), iw[:], bq[:, 2 * k, :],
                                                 ALU.subtract))
                    if k == 0:
                        chain.link(vec.tensor_scalar(iw[:], iw[:], 0.0, wr[:, 0:1], ALU.mult, ALU.add))
                vec.sem_inc(bias_done, 1)
                assert chain.n == bias_links

            def turn(r, last):
                first = isinstance(r, int) and r == 0
                chain = Chain(vec, dve, 0 if first else r * LINKS + bias_links)
                for n, (kind, u, part) in enumerate(plan):
                    if kind == V:
                        vec.wait_ge(acc_full, r * NPLAN + n + 1)
                        kt = (r & 1) * (KT // 2) + u * TPC + part
                        dst = v_all[:, bass.ds((r // 2) * H, H), bass.ds(kt, 1), :]
                        vec.tensor_copy(dst.rearrange("p h o d -> p (h o) d"),
                                        acc[n % 4][:].rearrange("p (h d) -> p h d", h=H)).then_inc(acc_free, 1)
                    else:
                        k = split_at.index(n)
                        vec.wait_ge(hi_done, r * NSPLIT + k + 1)
                        vec.scalar_tensor_tensor(out=lo[k % OUTB][:].bitcast(F32R), in0=acc[n % 4][:],
                                                 scalar=(SCALE if kind == Q else 1.0), in1=hi[k % OUTB][:],
                                                 op0=ALU.mult, op1=ALU.subtract).then_inc(acc_free, 1)
                    if n == SPLIT_V and first:
                        split_weights(V)
                    if n == SPLIT_Q and first:
                        split_weights(Q)
                    if n == STATS_AT:
                        vec.wait_ge(x_in, r * 16 + 16)
                        for s in range(TPC):
                            ins = vec.bn_stats(stats[:, s, :], xt[:, s, :])
                        chain.link(ins)
                        gate(vec, passed)
                        for s in range(TPC):
                            ins = vec.bn_aggr(mv[:, s, :], stats[:, s, :])
                        ins.then_inc(stats_done, 1)
                    if n == SPREAD_AT:
                        vec.wait_ge(sd_done, r + 1)
                        chain.link(vec.reciprocal(rstd[:], sd[:]))
                        vec.scalar_tensor_tensor(out=nmr[:], in0=mv[:, :, 0], scalar=-1.0, in1=rstd[:],
                                                 op0=ALU.mult, op1=ALU.mult).then_inc(scale_done, 1)
                    if TURN_AT <= n < TURN_AT + DC:
                        c = n - TURN_AT
                        vec.wait_ge(xt_hi_made, r * DC + c + 1)
                        vec.tensor_tensor(xt_lo[:, c, :].bitcast(F32R), tp[c % 2][:], xt_hi[:, c, :],
                                          ALU.subtract).then_inc(xt_lo_made, 1)

            split_weights(K)
            vec.wait_ge(ct_hi_made, 1)
            vec.tensor_tensor(ct_lo[0][:].bitcast(F32R), raw_ct[0], ct_hi[0][:], ALU.subtract).then_inc(ct_lo_made, 1)
            vec.memset(eps[:], EPS).then_inc(eps_done, 1)
            turns(vec, turn, bias_rows)


def attend(nc, qa_d, ka_d, bq_d, kc_d, m_d, v_all, ao, ident_in):
    with ExitStack() as ctx:
        sb, psum, sem = allocators(nc, ctx, "at")
        SLOTS = 4
        UNROLL = SLOTS
        HALF = TQ // 2
        STEPS = 2 * KT // 2
        HSTEPS = STEPS // 2
        LAG = 3
        PB = 4
        KC = TK // CH
        NM = QT * KC
        VW = 2 * DH + 1
        HQ = HALF // P
        SPLIT = 416
        TURN_MAX, COPY_OUT, TURN_OUT = 2, 3, 4
        MAKE_V = 5
        VPARTS = 4
        VK = KT // VPARTS
        VALUES_AT = 1
        ident = sb("ident", [P, P])
        qa = [sb(f"qa{u}", [P, TQ]) for u in range(SLOTS)]
        ka = [sb(f"ka{u}", [P, TK]) for u in range(SLOTS)]
        vs = [sb(f"vs{u}", [P, KT, VW]) for u in range(2)]
        pf = [sb(f"pf{u}", [P, 2 * HALF]) for u in range(2)]
        ph = [sb(f"ph{u}", [P, 2 * HALF]) for u in range(PB)]
        pl = [sb(f"pl{u}", [P, 2 * HALF]) for u in range(PB)]
        ot = [sb(f"ot{u}", [VW, HALF]) for u in range(2)]
        mpart = [sb(f"mpart{u}", [P, QT, KC]) for u in range(2)]
        mrow = sb("mrow", [P, QT])
        mx = sb("mx", [P, 2 * QT])
        mt = sb("mt", [2 * QT, P])
        oraw = sb("oraw", [P, HQ, VW])
        rsum = sb("rsum", [P, HQ])
        osum = sb("osum", [P, HQ, DH])
        s_ps = [psum(f"s_ps{u}", [P, 2 * HALF]) for u in range(2)]
        m_ps = [psum(f"m_ps{u}", [P, CH]) for u in range(2)]
        o_ps = [psum(f"o_ps{u}", [P, HALF]) for u in range(2)]

        ident_in_s = sem("ident_in")
        ones_made = sem("ones_made")
        rows_in = [sem(f"rows_in{u}") for u in range(SLOTS)]
        kq_in = [sem(f"kq_in{u}") for u in range(SLOTS)]
        v_hi = sem("v_hi")
        v_made = sem("v_made")
        m_full = sem("m_full")
        m_free = sem("m_free")
        mx_made = sem("mx_made")
        mt_made = sem("mt_made")
        mt_out = sem("mt_out")
        max_in = sem("max_in")
        s_full = sem("s_full")
        exp_done = sem("exp_done")
        hi_done = sem("hi_done")
        lo_vec = sem("lo_vec")
        lo_pool = sem("lo_pool")
        av_done = sem("av_done")
        ot_made = sem("ot_made")
        dve = sem("dve")
        passed = sem("passed")
        LOADS = 7

        def uses(u, n, first, last):
            for k in range(2 * n, 2 * n + 2):
                if not last or u < UNROLL - 2:
                    yield "max", k
            if n == TURN_MAX and not (last and u == UNROLL - 1):
                yield "turn", 0
            if n == TURN_OUT and not (first and u == 0):
                yield "out", 1
            if n == TURN_OUT + HSTEPS:
                yield "out", 0

        class Ring:

            def __init__(self, base, parity):
                self.base, self.parity, self.n = base, parity, 0

            def next(self):
                self.n += 1
                return self.base + self.n, (self.parity + self.n - 1) % 2

        BEFORE = 2 * (NM // 2) + 1
        FIRST = BEFORE + sum(len(list(uses(u, n, True, False))) for u in range(UNROLL) for n in range(STEPS))
        TURN = sum(len(list(uses(u, n, False, False))) for u in range(UNROLL) for n in range(STEPS))
        assert TURN % 2 == 0
        NTURN = NHEAD // UNROLL

        block = ctx.enter_context(nc.Block())

        @block.sync
        def _(sp):
            sp.dma_start(ident[:], ident_in).then_inc(ident_in_s, 16)
            def load(i, u):
                for k, part in enumerate((0, 1, 0)):
                    sp.dma_start(ka[u][k * DH:(k + 1) * DH, :],
                                 ka_d[part, bass.ds(i * DH, DH), :]).then_inc(kq_in[u], 16)
                for k, part in enumerate((0, 0, 1)):
                    sp.dma_start(qa[u][k * DH:(k + 1) * DH, :],
                                 qa_d[part, bass.ds(i * DH, DH), :]).then_inc(kq_in[u], 16)
                src = bq_d[:, bass.ds(i & (H - 1), 1), :].rearrange("r o t -> (r o) t")
                sp.dma_start(qa[u][BIAS0:MAX0, :], src).then_inc(kq_in[u], 16)

            def move_maxima(i, u):
                sp.wait_ge(mt_made, i + 1)
                sp.dma_start(m_d[u].rearrange("a (b t) -> (a b) t", t=P), mt[:]).then_inc(mt_out, 16)
                sp.wait_ge(mt_out, i * 16 + 16)
                sp.dma_start(qa[u][MAX0:KROWS, :], m_d[u]).then_inc(max_in, 16)

            for u in range(SLOTS):
                load(u, u)
                sp.dma_start(ka[u][BIAS0:KROWS, :], kc_d).then_inc(rows_in[u], 16)
            move_maxima(0, 0)
            with sp.Fori(0, NTURN - 1) as r:
                for u in range(SLOTS):
                    move_maxima(r * SLOTS + u + 1, (u + 1) % SLOTS)
                    sp.wait_ge(av_done, r * (SLOTS * STEPS) + (u + 1) * STEPS + PB)
                    load(r * SLOTS + u + SLOTS, u)
            for u in range(1, SLOTS):
                move_maxima(NHEAD - SLOTS + u, u)

        @block.gpsimd
        def _(pool):
            for u in range(2):
                pool.memset(vs[u][:, :, 2 * DH:VW], 1.0).then_inc(ones_made, 1)
                pool.wait_ge(ones_made, u + 1)


            def make_v_hi(i, u, q):
                pool.tensor_copy(vs[u % 2][:, q * VK:(q + 1) * VK, 0:DH].bitcast(F32R),
                                 v_all[:, bass.ds(i, 1), q * VK:(q + 1) * VK, :].rearrange("p o k d -> p (o k) d")
                                 ).then_inc(v_hi, 1)

            def make_v_lo(i, u, q):
                pool.wait_ge(v_hi, i * VPARTS + q + 1)
                gate(pool, passed)
                pool.tensor_tensor(vs[u % 2][:, q * VK:(q + 1) * VK, DH:2 * DH].bitcast(F32R),
                                   v_all[:, bass.ds(i, 1), q * VK:(q + 1) * VK, :].rearrange("p o k d -> p (o k) d"),
                                   vs[u % 2][:, q * VK:(q + 1) * VK, 0:DH], ALU.subtract).then_inc(v_made, 1)

            def head(j, u, last):
                for n in range(STEPS):
                    N = j * STEPS + n
                    pool.wait_ge(hi_done, N + 3)
                    pool.tensor_tensor(pl[n % PB][:, SPLIT:].bitcast(F32R), pf[n % 2][:, SPLIT:],
                                       ph[n % PB][:, SPLIT:], ALU.subtract).then_inc(lo_pool, 1)
                    if last:
                        continue
                    if n == MAKE_V:
                        pool.wait_ge(av_done, j * STEPS + PB)
                    q, half = divmod(n - MAKE_V, 2)
                    if 0 <= q < VPARTS:
                        (make_v_hi, make_v_lo)[half](j + 1, u + 1, q)

            for q in range(VPARTS):
                make_v_hi(0, 0, q)
                make_v_lo(0, 0, q)
            with pool.Fori(0, NTURN - 1) as r:
                for u in range(UNROLL):
                    head(r * UNROLL + u, u, False)
            for u in range(UNROLL):
                head(NHEAD - UNROLL + u, u, u == UNROLL - 1)

        @block.tensor
        def _(pe):
            def maximum(i, u, k, use, bank):
                qt, kc = k // KC, k % KC
                if k == 0:
                    pe.wait_ge(kq_in[u], (i // SLOTS) * (16 * LOADS) + 16 * LOADS)
                pe.wait_ge(m_free, use)
                pe.matmul(m_ps[bank][:], qa[u][0:MAX0, qt * P:(qt + 1) * P].bitcast(F32R),
                          ka[u][0:MAX0, kc * CH:(kc + 1) * CH].bitcast(F32R),
                          start=True, stop=True).then_inc(m_full, 1)

            def wide_maximum(i, k, use, bank):
                if k == 0:
                    pe.wait_ge(kq_in[i], 16 * LOADS)
                pe.wait_ge(m_free, use)
                for half in range(2):
                    qt, kc = (k + half) // KC, (k + half) % KC
                    last = pe.matmul(s_ps[bank][:, half * CH:(half + 1) * CH],
                                     qa[i][0:MAX0, qt * P:(qt + 1) * P].bitcast(F32R),
                                     ka[i][0:MAX0, kc * CH:(kc + 1) * CH].bitcast(F32R), start=True, stop=True)
                last.then_inc(m_full, 1)

            def turn_maxima(i, use, bank):
                pe.wait_ge(mx_made, i + 1)
                pe.wait_ge(m_free, use)
                pe.transpose(m_ps[bank][0:2 * QT, 0:P], mx[:], ident[:]).then_inc(m_full, 1)

            def turn_output(j, h, use, bank):
                pe.wait_ge(ot_made, j * 2 + h + 3)
                pe.wait_ge(m_free, use)
                for q in range(HQ):
                    last = pe.transpose(m_ps[bank][:, q * VW:(q + 1) * VW], ot[h][:, q * P:(q + 1) * P],
                                        ident[0:VW, 0:VW])
                last.then_inc(m_full, 1)

            def scores(j, u, n):
                h, kp = divmod(n, HSTEPS)
                if n == 0:
                    pe.wait_ge(max_in, j * 16 + 16)
                pe.wait_ge(hi_done, j * STEPS + n + 1)
                for k in range(2):
                    kt = 2 * kp + k
                    last = pe.matmul(s_ps[n % 2][:, k * HALF:(k + 1) * HALF],
                                     ka[u][0:KROWS, kt * P:(kt + 1) * P].bitcast(F32R),
                                     qa[u][0:KROWS, h * HALF:(h + 1) * HALF].bitcast(F32R), start=True, stop=True)
                last.then_inc(s_full, 1)

            def values(j, u, n):
                h, kp = divmod(n, HSTEPS)
                if n == 0:
                    pe.wait_ge(v_made, (j + 1) * VPARTS)
                if kp == 0:
                    pe.wait_ge(ot_made, j * 2 + h + 1)
                pe.wait_ge(lo_vec, j * STEPS + n + 3)
                pe.wait_ge(lo_pool, j * STEPS + n + 3)
                for k in range(2):
                    for part in (ph, pl):
                        last = pe.matmul(o_ps[h][0:VW, :], vs[u % 2][:, 2 * kp + k, :].bitcast(F32R),
                                         part[n % PB][:, k * HALF:(k + 1) * HALF].bitcast(F32R),
                                         start=(kp == 0 and k == 0 and part is ph),
                                         stop=(kp == HSTEPS - 1 and k == 1 and part is pl))
                last.then_inc(av_done, 1)

            def lagged(j, u, n):
                if isinstance(j, int) and j * STEPS + n < LAG:
                    return
                values(*((j, u, n - LAG) if n >= LAG else (j - 1, (u - 1) % UNROLL, n - LAG + STEPS)))

            def head(j, u, ring, first=False, last=False):
                for n in range(STEPS):
                    scores(j, u, n)
                    for pos, (kind, k) in enumerate(uses(u, n, first, last)):
                        if pos == VALUES_AT:
                            lagged(j, u, n)
                        if kind == "max":
                            maximum(j + 2, (u + 2) % SLOTS, k, *ring.next())
                        elif kind == "turn":
                            turn_maxima(j + 1, *ring.next())
                        else:
                            turn_output(j - k, k, *ring.next())
                    if len(list(uses(u, n, first, last))) <= VALUES_AT:
                        lagged(j, u, n)

            pe.wait_ge(ident_in_s, 16)
            ring = Ring(0, 0)
            for i in range(2):
                pe.wait_ge(rows_in[i], 16)
                for k in range(0, NM, 2):
                    wide_maximum(i, k, *ring.next())
                if i == 0:
                    turn_maxima(0, *ring.next())
            for u in range(2, SLOTS):
                pe.wait_ge(rows_in[u], 16)
            pe.wait_ge(m_free, ring.n + 2)
            for u in range(UNROLL):
                head(u, u, ring, first=True)
            assert ring.n == FIRST
            with pe.Fori(1, NTURN - 1) as r:
                ring = Ring(r * TURN + (FIRST - TURN), FIRST % 2)
                for u in range(UNROLL):
                    head(r * UNROLL + u, u, ring)
            ring = Ring(FIRST + (NTURN - 2) * TURN, FIRST % 2)
            for u in range(UNROLL):
                head(NHEAD - UNROLL + u, u, ring, last=True)
            for n in range(STEPS - LAG, STEPS):
                values(NHEAD - 1, UNROLL - 1, n)
            turn_output(NHEAD - 1, 1, *ring.next())

        @block.scalar
        def _(act):
            act.nop().then_inc(hi_done, 2)
            act.nop().then_inc(ot_made, 2)

            def copy_output(j, h):
                act.wait_ge(av_done, j * STEPS + (h + 1) * HSTEPS + PB)
                act.activation(ot[h][:], o_ps[h][0:VW, :], ACT.Copy).then_inc(ot_made, 1)

            def head(j, u, first=False):
                for n in range(STEPS):
                    N = j * STEPS + n
                    act.wait_ge(s_full, N + 1)
                    act.wait_ge(lo_vec, N + 1)
                    act.wait_ge(lo_pool, N + 1)
                    act.activation(pf[n % 2][:], s_ps[n % 2][:], ACT.Exp).then_inc(exp_done, 1)
                    act.wait_ge(av_done, N + 1)
                    act.activation(ph[n % PB][:].bitcast(F32R), s_ps[n % 2][:], ACT.Exp).then_inc(hi_done, 1)
                    if n == COPY_OUT and not (first and u == 0):
                        copy_output(j - 1, 1)
                    if n == COPY_OUT + HSTEPS:
                        copy_output(j, 0)

            for u in range(UNROLL):
                head(u, u, first=True)
            with act.Fori(1, NTURN) as r:
                for u in range(UNROLL):
                    head(r * UNROLL + u, u)
            copy_output(NHEAD - 1, 1)

        @block.vector
        def _(vec):
            vec.nop().then_inc(m_free, 2)
            vec.nop().then_inc(av_done, PB)
            vec.nop().then_inc(lo_vec, 2)
            vec.nop().then_inc(lo_pool, 2)

            def maximum(u, k, use, bank):
                vec.wait_ge(m_full, use)
                vec.tensor_reduce(mpart[u % 2][:, k // KC, k % KC:k % KC + 1], m_ps[bank][:], AX.X, ALU.max)\
                   .then_inc(m_free, 1)

            def wide_maximum(i, k, use, bank):
                vec.wait_ge(m_full, use)
                vec.tensor_reduce(mpart[i % 2][:, k // KC, k % KC:k % KC + 2],
                                  s_ps[bank][:].rearrange("p (h t) -> p h t", h=2), AX.X, ALU.max).then_inc(m_free, 1)

            def row_maximum(u, use, chain):
                vec.wait_ge(m_free, use + 2)
                chain.mark(vec.tensor_reduce(mrow[:], mpart[u % 2][:], AX.X, ALU.max))

            def mx_high(chain):
                chain.settle()
                chain.mark(vec.tensor_scalar(mx[:, 0:QT].bitcast(F32R), mrow[:], -1.0, None, ALU.mult))

            def mx_low(chain):
                chain.settle()
                vec.scalar_tensor_tensor(out=mx[:, QT:2 * QT].bitcast(F32R), in0=mrow[:], scalar=-1.0,
                                         in1=mx[:, 0:QT], op0=ALU.mult, op1=ALU.subtract).then_inc(mx_made, 1)

            def copy_maxima(i, use, bank, any_before=True):
                vec.wait_ge(m_full, use)
                if any_before:
                    vec.wait_ge(mt_out, i * 16)
                vec.tensor_copy(mt[:], m_ps[bank][0:2 * QT, 0:P]).then_inc(m_free, 1)
                vec.wait_ge(m_free, use + 2)
                vec.sem_inc(mt_made, 1)

            def take_output(use, bank):
                vec.wait_ge(m_full, use)
                vec.tensor_copy(oraw[:], m_ps[bank][:, 0:HQ * VW].rearrange("p (q d) -> p q d", q=HQ)).then_inc(m_free, 1)

            def add_output(use, chain):
                vec.wait_ge(m_free, use + 2)
                chain.mark(vec.reciprocal(rsum[:], oraw[:, :, 2 * DH]))
                chain.mark(vec.tensor_tensor(osum[:], oraw[:, :, 0:DH], oraw[:, :, DH:2 * DH], ALU.add))

            def divide_output(j, h, chain):
                chain.settle()
                dst = ao[:, bass.ds(j, 1), h * HQ:(h + 1) * HQ, :].rearrange("p o q d -> p (o q) d")
                chain.mark(vec.tensor_tensor(dst, osum[:], rsum[:].unsqueeze(2).to_broadcast([P, HQ, DH]), ALU.mult))

            def low(j, n):
                vec.wait_ge(hi_done, j * STEPS + n + 3)
                vec.tensor_tensor(pl[n % PB][:, 0:SPLIT].bitcast(F32R), pf[n % 2][:, 0:SPLIT],
                                  ph[n % PB][:, 0:SPLIT], ALU.subtract).then_inc(lo_vec, 1)

            def head(j, u, ring, chain, first=False, last=False):
                maxima = not last or u < UNROLL - 2
                makes_mx = not (first and u == 0) and not (last and u == UNROLL - 1)
                for n in range(STEPS):
                    if maxima:
                        maximum(u, 2 * n, *ring.next())
                    if n == 0 and makes_mx:
                        row_maximum(u - 1, ring.base + ring.n - maxima, chain)
                    if not (first and u == 0 and n == 0):
                        low(*((j, n - 1) if n else (j - 1, STEPS - 1)))
                    if n == 0 and makes_mx:
                        mx_high(chain)
                    for h, at in ((1, TURN_OUT + 1), (0, TURN_OUT + 1 + HSTEPS)):
                        if n == at and not (first and u == 0 and h == 1):
                            add_output(taken, chain)
                    if maxima:
                        maximum(u, 2 * n + 1, *ring.next())
                    if n == 0 and makes_mx:
                        mx_low(chain)
                    for h, at in ((1, TURN_OUT + 1), (0, TURN_OUT + 1 + HSTEPS)):
                        if n == at and not (first and u == 0 and h == 1):
                            divide_output(j - h, h, chain)
                    for kind, k in uses(u, n, first, last):
                        if kind == "turn":
                            copy_maxima(j + 1, *ring.next())
                        if kind == "out":
                            taken, bank = ring.next()
                            take_output(taken, bank)

            chain = Chain(vec, dve)
            ring = Ring(0, 0)
            for i in range(2):
                for k in range(0, NM, 2):
                    use, bank = ring.next()
                    wide_maximum(i, k, use, bank)
                row_maximum(i, use, chain)
                mx_high(chain)
                mx_low(chain)
                if i == 0:
                    copy_maxima(0, *ring.next(), any_before=False)
            for u in range(UNROLL):
                head(u, u, ring, chain, first=True)
            base = chain.n
            PER_TURN = UNROLL * (2 + 2 * 3)
            with vec.Fori(1, NTURN - 1) as r:
                ring = Ring(r * TURN + (FIRST - TURN), FIRST % 2)
                chain = Chain(vec, dve, r * PER_TURN + (base - PER_TURN))
                for u in range(UNROLL):
                    head(r * UNROLL + u, u, ring, chain)
                assert chain.n == PER_TURN
            ring = Ring(FIRST + (NTURN - 2) * TURN, FIRST % 2)
            chain = Chain(vec, dve, base + (NTURN - 2) * PER_TURN)
            for u in range(UNROLL):
                head(NHEAD - UNROLL + u, u, ring, chain, last=True)
            low(NHEAD - 1, STEPS - 1)
            taken, bank = ring.next()
            take_output(taken, bank)
            add_output(taken, chain)
            divide_output(NHEAD - 1, 1, chain)


def mix(nc, x, w_proj, w_q, ident_in, ao, x2_d, xn_d, q_d, mvq):
    with ExitStack() as ctx:
        sb, psum, sem = allocators(nc, ctx, "mx")
        NCH = B * TQ // CH
        QG = 4
        ident = sb("ident", [P, P])
        wp = sb("wp", [P, DC, D])
        wq_hi = sb("wq_hi", [P, DC, QC * P])
        wq_lo = sb("wq_lo", [P, DC, QC * P])
        xt = sb("xt", [P, 2 * TPC, D])
        at = [sb(f"at{u}", [P, D]) for u in range(2)]
        att = [sb(f"att{u}", [P, D]) for u in range(2)]
        x2 = [sb(f"x2{u}", [P, D]) for u in range(2)]
        xn = [sb(f"xn{u}", [P, D]) for u in range(2)]
        xh = sb("xh", [P, 2, DC, CH])
        xl = sb("xl", [P, 2, DC, CH])
        qs = [sb(f"qs{u}", [P, TPC, QG, P]) for u in range(QC // QG)]
        st = sb("st", [P, 6])
        mv = sb("mv", [P, 2])
        sd = sb("sd", [P, 1])
        rstd = sb("rstd", [P, 1])
        nmr = sb("nmr", [P, 1])
        eps = sb("eps", [P, 1])
        stq = sb("stq", [P, QC, NCH, 6])
        tp = [psum(f"tp{u}", [P, CH]) for u in range(2)]
        yp = [psum(f"yp{u}", [P, CH]) for u in range(2)]
        qp = [psum(f"qp{u}", [P, CH]) for u in range(4)]

        ident_here = sem("ident_here")
        wp_in = sem("wp_in")
        wq_in = [sem(f"wq_in{d}") for d in range(DC)]
        w_hi_made = sem("w_hi_made")
        w_lo_made = sem("w_lo_made")
        x_in = sem("x_in")
        at_made = sem("at_made")
        at_turned = sem("at_turned")
        att_made = sem("att_made")
        y_full = sem("y_full")
        x2_made = sem("x2_made")
        stats_done = sem("stats_done")
        sd_done = sem("sd_done")
        scale_done = sem("scale_done")
        xn_made = sem("xn_made")
        xn_turned = sem("xn_turned")
        xh_made = sem("xh_made")
        xl_made = sem("xl_made")
        q_full = sem("q_full")
        q_copied = sem("q_copied")
        q_counted = sem("q_counted")
        rows_out = [sem(f"rows_out{u}") for u in range(2)]
        q_out = [sem(f"q_out{u}") for u in range(QC // QG)]
        eps_done = sem("eps_done")
        passed = sem("passed")
        dve = sem("dve")

        def chunks(eng, front_part, query, prepare=None):
            def step(c):
                for k in range(QC):
                    query(c, k)
                    front_part(c + 1, k)

            for k in range(QC):
                front_part(0, k)
                if prepare:
                    prepare(k)
            step(0)
            with eng.Fori(1, NCH - 1) as c:
                step(c)
            for k in range(QC):
                query(NCH - 1, k)

        TURN_AT, OUT_AT, TURN_XN = (0, 2, 5, 8), (1, 3, 6, 9), (4, 7, 10, 13)
        COPY_AT, SPREAD, COPY_XN = (0, 2, 5, 8), (2, 4, 7, 10), (4, 7, 10, 13)
        NORM, LOW = (2, 4, 7, 10), (4, 7, 10, 13)
        SPLIT_W = (2, 5, 8, 13)

        block = ctx.enter_context(nc.Block())

        @block.sync
        def _(sp):
            x_v = x.rearrange("b (n p) d -> p (b n) d", p=P)

            def load_x(c):
                wait_count(sp, x2_made, (c - 1) * TPC)
                gate(sp, passed)
                sp.dma_start(xt[:, bass.ds((c & 1) * TPC, TPC), :],
                             x_v[:, bass.ds(c * TPC, TPC), :]).then_inc(x_in, 16)

            def store_rows(c, s):
                sp.wait_ge(xn_made, c * TPC + s + 1)
                rows = bass.ds(c * CH + s * P, P)
                sp.dma_start(x2_d[rows, :], x2[s % 2][:]).then_inc(rows_out[s % 2], 16)
                sp.dma_start(xn_d[rows, :], xn[s % 2][:]).then_inc(rows_out[s % 2], 16)

            def store_queries(c, g):
                sp.wait_ge(q_copied, c * QC + QG * g + QG)
                dst = q_d[bass.ds(c * TPC, TPC), :, QG * g:QG * g + QG, :]
                sp.dma_start(dst.rearrange("s p k t -> p s (k t)"),
                             qs[g][:].rearrange("p s k t -> p s (k t)")).then_inc(q_out[g], 16)

            def step(c):
                load_x(c + 1)
                for g in range(QC // QG):
                    if g:
                        store_rows(c + 1, g - 1)
                    store_queries(c, g)
                store_rows(c + 1, TPC - 1)

            sp.dma_start(ident[:], ident_in).then_inc(ident_here, 16)
            sp.dma_start(wp[:], w_proj.rearrange("(c p) e -> p c e", p=P)).then_inc(wp_in, 16)
            load_x(0)
            for d in range(DC):
                sp.dma_start(qs[d][:].rearrange("p s k t -> p (s k t)"),
                             w_q[d * P:(d + 1) * P, :]).then_inc(wq_in[d], 16)
            for s in range(TPC):
                store_rows(0, s)
            step(0)
            with sp.Fori(1, NCH - 1) as c:
                step(c)
            for g in range(QC // QG):
                store_queries(NCH - 1, g)
            for u in range(2):
                sp.wait_ge(rows_out[u], 32 * NT // 2)
            for g in range(QC // QG):
                sp.wait_ge(q_out[g], 16 * NCH)

        @block.gpsimd
        def _(pool):
            def gather_heads(c):
                for s in range(TPC):
                    t = c * TPC + s
                    wait_count(pool, at_turned, t - 1)
                    src = ao[:, bass.ds((c // 2) * H, H), bass.ds((c & 1) * TPC + s, 1), :]
                    pool.tensor_copy(at[s % 2][:].rearrange("p (h d) -> p h d", h=H),
                                     src.rearrange("p h o d -> p h (o d)")).then_inc(at_made, 1)

            gather_heads(0)
            with pool.Fori(1, NCH) as c:
                gather_heads(c)

        @block.tensor
        def _(pe):
            def turn_attended(c, s):
                t = c * TPC + s
                pe.wait_ge(at_made, t + 1)
                wait_count(pe, att_made, t)
                for d in range(DC):
                    last = pe.transpose(tp[0][:, d * P:(d + 1) * P], at[s % 2][:, d * P:(d + 1) * P], ident[:])
                last.then_inc(at_turned, 1)

            def output(c, s):
                t = c * TPC + s
                pe.wait_ge(att_made, t + 1)
                pe.wait_ge(wp_in, 16)
                wait_count(pe, x2_made, t - 1)
                for d in range(DC):
                    last = pe.matmul(yp[s % 2][:], att[s % 2][:, d * P:(d + 1) * P], wp[:, d, :],
                                     start=(d == 0), stop=(d == DC - 1))
                last.then_inc(y_full, 1)

            def turn_normed(c, s):
                t = c * TPC + s
                pe.wait_ge(xn_made, t + 1)
                wait_count(pe, xl_made, t)
                for d in range(DC):
                    last = pe.transpose(tp[1][:, d * P:(d + 1) * P], xn[s % 2][:, d * P:(d + 1) * P], ident[:])
                last.then_inc(xn_turned, 1)

            def front_part(c, k):
                for part, places in ((turn_attended, TURN_AT), (output, OUT_AT), (turn_normed, TURN_XN)):
                    if k in places:
                        part(c, places.index(k))

            def query(c, k):
                if k == 0:
                    pe.wait_ge(xl_made, (c + 1) * TPC)
                wait_count(pe, q_copied, c * QC + k - 3)
                for d in range(DC):
                    if k == 0 and isinstance(c, int) and c == 0:
                        pe.wait_ge(w_lo_made, d + 1)
                    for w_part, x_part in ((wq_hi, xh), (wq_hi, xl), (wq_lo, xh)):
                        last = pe.matmul(qp[k % 4][:], w_part[:, d, k * P:(k + 1) * P].bitcast(F32R),
                                         x_part[:, bass.ds(c & 1, 1), d, :].rearrange("p o t -> p (o t)").bitcast(F32R),
                                         start=(d == 0 and w_part is wq_hi and x_part is xh),
                                         stop=(d == DC - 1 and w_part is wq_lo))
                last.then_inc(q_full, 1)

            pe.wait_ge(ident_here, 16)
            chunks(pe, front_part, query)

        @block.scalar
        def _(act):
            def copy_attended(c, s):
                t = c * TPC + s
                act.wait_ge(at_turned, t + 1)
                wait_count(act, y_full, t - 1)
                act.activation(att[s % 2][:], tp[0][:], ACT.Copy).then_inc(att_made, 1)

            def spread(c, s):
                act.wait_ge(stats_done, c * TPC + s + 1)
                act.activation(sd[:], mv[:, 1:2], ACT.Sqrt, bias=eps[:]).then_inc(sd_done, 1)

            def copy_normed(c, s):
                act.wait_ge(xn_turned, c * TPC + s + 1)
                if s == 0:
                    wait_count(act, q_full, (c - 1) * QC)
                act.activation(xh[:, bass.ds(c & 1, 1), :, s * P:(s + 1) * P].rearrange("p o d t -> p (o d) t").bitcast(F32R),
                               tp[1][:].rearrange("p (d t) -> p d t", d=DC), ACT.Copy).then_inc(xh_made, 1)

            def front_part(c, k):
                for part, places in ((copy_attended, COPY_AT), (spread, SPREAD), (copy_normed, COPY_XN)):
                    if k in places:
                        part(c, places.index(k))

            def prepare(k):
                if k in SPLIT_W:
                    d = SPLIT_W.index(k)
                    act.wait_ge(wq_in[d], 16)
                    act.activation(wq_hi[:, d, :].bitcast(F32R), qs[d][:].rearrange("p s k t -> p (s k t)"),
                                   ACT.Copy).then_inc(w_hi_made, 1)

            def query(c, k):
                act.wait_ge(q_full, c * QC + k + 1)
                if k % QG == 0:
                    wait_count(act, q_out[k // QG], 16 * c)
                    wait_count(act, q_counted, (c - 1) * QC + k + QG)
                act.activation(qs[k // QG][:, :, k % QG, :], qp[k % 4][:].rearrange("p (s t) -> p s t", s=TPC),
                               ACT.Copy).then_inc(q_copied, 1)

            act.wait_ge(eps_done, 1)
            chunks(act, front_part, query, prepare)

        @block.vector
        def _(vec):
            LINKS = 2

            def norm(c, s):
                t = c * TPC + s
                chain = Chain(vec, dve, t * LINKS)
                if s == 0:
                    vec.wait_ge(x_in, c * 16 + 16)
                vec.wait_ge(y_full, t + 1)
                wait_count(vec, rows_out[s % 2], c * (16 * TPC) + 32 * (s // 2))
                wait_count(vec, xn_turned, t - 1)
                vec.tensor_tensor(x2[s % 2][:], yp[s % 2][:],
                                  xt[:, bass.ds((c & 1) * TPC + s, 1), :].rearrange("p o d -> p (o d)"),
                                  ALU.add).then_inc(x2_made, 1)
                vec.wait_ge(x2_made, t + 1)
                chain.link(vec.bn_stats(st[:], x2[s % 2][:]))
                gate(vec, passed)
                vec.bn_aggr(mv[:], st[:]).then_inc(stats_done, 1)
                vec.wait_ge(sd_done, t + 1)
                chain.link(vec.reciprocal(rstd[:], sd[:]))
                vec.scalar_tensor_tensor(out=nmr[:], in0=mv[:, 0:1], scalar=-1.0, in1=rstd[:],
                                         op0=ALU.mult, op1=ALU.mult).then_inc(scale_done, 1)
                vec.wait_ge(scale_done, t + 1)
                vec.tensor_scalar(xn[s % 2][:], x2[s % 2][:], rstd[:], nmr[:], ALU.mult,
                                  ALU.add).then_inc(xn_made, 1)

            def low(c, s):
                vec.wait_ge(xh_made, c * TPC + s + 1)
                here = bass.ds(c & 1, 1), slice(None), slice(s * P, (s + 1) * P)
                vec.tensor_tensor(xl[(slice(None), *here)].rearrange("p o d t -> p (o d) t").bitcast(F32R),
                                  tp[1][:].rearrange("p (d t) -> p d t", d=DC),
                                  xh[(slice(None), *here)].rearrange("p o d t -> p (o d) t"),
                                  ALU.subtract).then_inc(xl_made, 1)

            def front_part(c, k):
                for part, places in ((norm, NORM), (low, LOW)):
                    if k in places:
                        part(c, places.index(k))

            def prepare(k):
                if k in SPLIT_W:
                    d = SPLIT_W.index(k)
                    vec.wait_ge(w_hi_made, d + 1)
                    vec.tensor_tensor(wq_lo[:, d, :].bitcast(F32R), qs[d][:].rearrange("p s k t -> p (s k t)"),
                                      wq_hi[:, d, :], ALU.subtract).then_inc(w_lo_made, 1)

            def query(c, k):
                vec.wait_ge(q_copied, c * QC + k + 1)
                vec.bn_stats(stq[:, k, bass.ds(c, 1), :].rearrange("p o s -> p (o s)"),
                             qs[k // QG][:, :, k % QG, :]).then_inc(q_counted, 1)

            vec.memset(eps[:], EPS).then_inc(eps_done, 1)
            chunks(vec, front_part, query, prepare)
            vec.wait_ge(q_counted, NCH * QC)
            for k in range(QC):
                vec.bn_aggr(mvq[:, k, :], stq[:, k, :, :].rearrange("p g s -> p (g s)"))


def experts(nc, table, keys_t, gamma_t, beta_t, ident_in, mvq, x2_d, xn_d, q_d, out):
    with ExitStack() as ctx:
        sb, psum, sem = allocators(nc, ctx, "ex")
        RG = 4
        ident = sb("ident", [P, P])
        keys = sb("keys", [P, QC, NKEY])
        gam = sb("gam", [P, QC])
        bet = sb("bet", [P, QC])
        eps = sb("eps", [P, 1])
        qsc = sb("qsc", [P, QC])
        qbi = sb("qbi", [P, QC])
        qt = sb("qt", [P, QC, P])
        qn = sb("qn", [P, QC, P])
        xn = [sb(f"xn{u}", [P, D]) for u in range(2)]
        x2 = [sb(f"x2{u}", [P, D]) for u in range(2)]
        yo = sb("yo", [P, D])
        ring = [sb(f"ring{g}", [P, TOPK, EW]) for g in range(RG)]
        diag = [sb(f"diag{k}", [P, P]) for k in range(TOPK)]
        eight_i = sb("eight_i", [P, TOPK], I32)
        eight = sb("eight", [P, TOPK])
        top = sb("top", [P, QC, TOPK])
        pos = sb("pos", [P, QC, TOPK], U32)
        posf = sb("posf", [P, QC, TOPK])
        cand = sb("cand", [P, PH, TOPK * TOPK])
        best = sb("best", [P, PH, TOPK])
        pick = sb("pick", [P, 2, NSLOT], U32)
        pickf = sb("pickf", [P, 2, NSLOT])
        hot = sb("hot", [P, NSLOT, TOPK])
        sel = sb("sel", [P, 2, NSLOT])
        idx = [sb(f"idx{u}", [P, NSLOT], U32) for u in range(2)]
        shifted = sb("shifted", [P, PH, TOPK])
        expd = sb("expd", [P, PH, TOPK])
        esum = sb("esum", [P, PH])
        wgt = [sb(f"wgt{u}", [P, PH, TOPK]) for u in range(2)]
        hid = sb("hid", [P, TOPK])
        g1 = sb("g1", [P, TOPK])
        g2 = sb("g2", [P, TOPK])
        g3 = sb("g3", [P, TOPK])
        g4 = sb("g4", [P, TOPK])
        wh = sb("wh", [P, TOPK])
        coef = sb("coef", [P, TOPK])
        sim = [psum(f"sim{u}", [P, 4, NKEY]) for u in range(4)]
        acc = [psum(f"acc{u}", [P, D]) for u in range(2)]

        consts_in = sem("consts_in")
        affine_in = sem("affine_in")
        q_in = sem("q_in")
        x_in = [sem(f"x_in{u}") for u in range(2)]
        qn_made = sem("qn_made")
        sim_made = sem("sim_made")
        sim_read = sem("sim_read")
        shift_made = sem("shift_made")
        exp_made = sem("exp_made")
        routed = sem("routed")
        rows_in = [sem(f"rows_in{g}") for g in range(RG)]
        arg_made = sem("arg_made")
        gelu_exp = sem("gelu_exp")
        coef_made = sem("coef_made")
        diag_made = sem("diag_made")
        diag_used = sem("diag_used")
        y_made = sem("y_made")
        y_out = sem("y_out")
        qsd_made = sem("qsd_made")
        aff_made = sem("aff_made")
        eight_made = sem("eight_made")
        passed = sem("passed")
        mv_ready = sem("mv_ready")
        dve = sem("dve")

        ROUTE_LINKS = 17
        GROUP_LINKS = TOPK + 6
        TILE_LINKS = ROUTE_LINKS + PH * GROUP_LINKS

        block = ctx.enter_context(nc.Block())

        @block.sync
        def _(sp):
            sp.dma_start(gam[:], gamma_t).then_inc(affine_in, 16)
            sp.dma_start(bet[:], beta_t).then_inc(affine_in, 16)

            def load(t, u):
                sp.dma_start(qt[:].rearrange("p c t -> p (c t)"),
                             q_d[bass.ds(t, 1), :, :, :].rearrange("o p c t -> (o p) (c t)")).then_inc(q_in, 16)
                sp.dma_start(xn[u][:], xn_d[bass.ds(t * P, P), :]).then_inc(x_in[u], 16)
                sp.dma_start(x2[u][:], x2_d[bass.ds(t * P, P), :]).then_inc(x_in[u], 16)

            def tile(t, u):
                sp.wait_ge(qn_made, t * QC + QC)
                wait_count(sp, y_made, t)
                load(t + 1, 1 - u)

            def store(t):
                sp.wait_ge(y_made, t + 1)
                sp.dma_start(out[bass.ds(t * P, P), :], yo[:]).then_inc(y_out, 16)

            load(0, 0)
            sp.dma_start(keys[:], keys_t).then_inc(consts_in, 16)
            sp.dma_start(ident[:], ident_in).then_inc(consts_in, 16)
            for u in range(2):
                tile(u, u)
                store(u)
            with sp.Fori(1, NT // 2 - 1) as r:
                for u in range(2):
                    tile(r * 2 + u, u)
                    store(r * 2 + u)
            tile(NT - 2, 0)
            store(NT - 2)
            store(NT - 1)
            sp.wait_ge(y_out, 16 * NT)

        @block.gpsimd
        def _(pool):
            pool.iota(eight_i[:], pattern=[[1, TOPK]], base=0, channel_multiplier=0).then_inc(eight_made, 1)
            with pool.Fori(0, NT // 2) as r:
                for u in range(2):
                    pool.wait_ge(routed, r * 2 + u + 1)
                    for g in range(PH):
                        pool.wait_ge(diag_used, r * (2 * PH) + u * PH + g + 1)
                        gate(pool, passed)
                        for k in range(TOPK):
                            n = g * TOPK + k
                            pool.indirect_dma_start(
                                ring[g % RG][:, k, :], None, table,
                                bass.IndirectOffsetOnAxis(ap=idx[u][:, n:n + 1], axis=0),
                            ).then_inc(rows_in[g % RG], 16)

        @block.tensor
        def _(pe):
            pe.wait_ge(consts_in, 32)

            def similar(t):
                wait_count(pe, sim_read, t)
                for c in range(QC):
                    pe.wait_ge(qn_made, t * QC + c + 1)
                    last = pe.matmul(sim[c // 4][:, c % 4, :], qn[:, c, :], keys[:, c, :], start=True, stop=True)
                last.then_inc(sim_made, 1)

            def group(t, u, g):
                if g == 0:
                    wait_count(pe, y_made, t - 1)
                pe.wait_ge(rows_in[g % RG], t * (PH // RG * TOPK * 16) + (g // RG + 1) * TOPK * 16)
                for k in range(TOPK):
                    pe.wait_ge(diag_made, t * NSLOT + g * TOPK + k + 1)
                    last = pe.matmul(acc[u][:], diag[k][:], ring[g % RG][:, k, D:EW],
                                     start=(g == 0 and k == 0), stop=(g == PH - 1 and k == TOPK - 1))
                last.then_inc(diag_used, 1)

            def tile(t, u, routes=True):
                for g in range(PH):
                    if g == 3 and routes:
                        similar(t + 1)
                    group(t, u, g)

            similar(0)
            for u in range(2):
                tile(u, u)
            with pe.Fori(1, NT // 2 - 1) as r:
                for u in range(2):
                    tile(r * 2 + u, u)
            tile(NT - 2, 0)
            tile(NT - 1, 1, routes=False)

        @block.scalar
        def _(act):
            act.wait_ge(aff_made, 1)
            act.activation(qsc[:], mvq[:, :, 1], ACT.Sqrt, bias=eps[:]).then_inc(qsd_made, 1)
            act.wait_ge(aff_made, 2)

            def affine(t):
                act.wait_ge(q_in, t * 16 + 16)
                wait_count(act, sim_made, t)
                for c in range(QC):
                    act.activation(qn[:, c, :], qt[:, c, :], ACT.Identity, bias=qbi[:, c:c + 1],
                                   scale=qsc[:, c:c + 1]).then_inc(qn_made, 1)

            def weights(t):
                act.wait_ge(shift_made, t + 1)
                act.activation(expd[:], shifted[:], ACT.Exp).then_inc(exp_made, 1)

            def group(t, g):
                n = t * PH + g
                act.wait_ge(arg_made, n + 1)
                act.activation(g4[:], g3[:], ACT.Exp).then_inc(gelu_exp, 1)
                act.wait_ge(coef_made, n + 1)
                act.wait_ge(diag_used, n + RG)
                for k in range(TOPK):
                    act.activation(diag[k][:], ident[:], ACT.Copy, scale=coef[:, k:k + 1]).then_inc(diag_made, 1)

            def tile(t, routes=True):
                for g in range(PH):
                    if g == 2 and routes:
                        affine(t + 1)
                    group(t, g)
                    if g == 3 and routes:
                        weights(t + 1)

            affine(0)
            weights(0)
            act.wait_ge(consts_in, 32)
            tile(0)
            with act.Fori(1, NT - 1) as t:
                tile(t)
            tile(NT - 1, routes=False)

        @block.vector
        def _(vec):
            chain = Chain(vec, dve)
            vec.nop().then_inc(diag_used, RG)
            chain.mark(vec.memset(eps[:], EPS))
            chain.settle()
            vec.nop().then_inc(aff_made, 1)
            vec.wait_ge(eight_made, 1)
            vec.wait_ge(affine_in, 32)
            chain.mark(vec.tensor_copy(eight[:], eight_i[:]))
            vec.wait_ge(qsd_made, 1)
            chain.link(vec.reciprocal(qbi[:], qsc[:]))
            chain.link(vec.tensor_tensor(qsc[:], qbi[:], gam[:], ALU.mult))
            chain.link(vec.tensor_tensor(qbi[:], mvq[:, :, 0], qsc[:], ALU.mult))
            vec.tensor_tensor(qbi[:], bet[:], qbi[:], ALU.subtract).then_inc(aff_made, 1)

            def route(t, u, chain):
                start = chain.n
                vec.wait_ge(sim_made, t + 1)
                gate(vec, passed)
                for c in range(QC):
                    last = vec.max(top[:, c, :], sim[c // 4][:, c % 4, :])
                chain.link(last)
                gate(vec, passed)
                for c in range(QC):
                    last = vec.max_index(pos[:, c, :], top[:, c, :], sim[c // 4][:, c % 4, :])
                last.then_inc(sim_read, 1)
                vec.wait_ge(sim_read, t + 1)
                chain.mark(vec.tensor_copy(posf[:], pos[:]))
                pair = [P, PH, TOPK, TOPK]
                chain.link(vec.tensor_tensor(cand[:].rearrange("p h (a b) -> p h a b", a=TOPK),
                                             top[:, 0:PH, :].unsqueeze(3).to_broadcast(pair),
                                             top[:, PH:QC, :].unsqueeze(2).to_broadcast(pair), ALU.add))
                gate(vec, passed)
                for h in range(PH):
                    last = vec.max(best[:, h, :], cand[:, h, :])
                chain.link(last)
                gate(vec, passed)
                for h in range(PH):
                    last = vec.max_index(pick[:, 0, h * TOPK:(h + 1) * TOPK], best[:, h, :], cand[:, h, :])
                chain.link(last)
                vec.tensor_tensor(shifted[:], best[:], best[:, :, 0:1].to_broadcast([P, PH, TOPK]),
                                  ALU.subtract).then_inc(shift_made, 1)
                chain.link(vec.tensor_scalar(pick[:, 1, :], pick[:, 0, :], 7, None, ALU.bitwise_and))
                chain.link(vec.tensor_scalar(pick[:, 0, :], pick[:, 0, :], 3, None, ALU.logical_shift_right))
                chain.link(vec.tensor_copy(pickf[:], pick[:]))
                for side in range(2):
                    chain.link(vec.tensor_tensor(
                        hot[:], pickf[:, side, :].unsqueeze(2).to_broadcast([P, NSLOT, TOPK]),
                        eight[:].unsqueeze(1).to_broadcast([P, NSLOT, TOPK]), ALU.is_equal))
                    hot4 = hot[:].rearrange("p (h k) a -> p h k a", h=PH)
                    chain.link(vec.tensor_tensor(
                        hot4, hot4, posf[:, side * PH:(side + 1) * PH, :].unsqueeze(2).to_broadcast(pair), ALU.mult))
                    chain.link(vec.tensor_reduce(sel[:, side, :], hot[:], AX.X, ALU.add))
                vec.scalar_tensor_tensor(out=idx[u][:], in0=sel[:, 0, :], scalar=float(NKEY), in1=sel[:, 1, :],
                                         op0=ALU.mult, op1=ALU.add).then_inc(routed, 1)
                vec.wait_ge(exp_made, t + 1)
                chain.link(vec.tensor_reduce(esum[:], expd[:], AX.X, ALU.add))
                chain.link(vec.reciprocal(esum[:], esum[:]))
                chain.mark(vec.tensor_tensor(wgt[u][:], expd[:], esum[:].unsqueeze(2).to_broadcast([P, PH, TOPK]),
                                             ALU.mult))
                assert chain.n == start + ROUTE_LINKS

            def group(t, u, g, chain):
                start = chain.n
                if g == 0:
                    vec.wait_ge(x_in[u], (t // 2) * 32 + 32)
                vec.wait_ge(rows_in[g % RG], t * (PH // RG * TOPK * 16) + (g // RG + 1) * TOPK * 16)
                for k in range(TOPK):
                    down = ring[g % RG][:, k, 0:D]
                    chain.mark(vec.tensor_tensor_reduce(down, down, xn[u][:], 1.0, 0.0,
                                                        ALU.mult, ALU.add, hid[:, k:k + 1]))
                chain.settle()
                chain.link(vec.tensor_tensor(g1[:], hid[:], hid[:], ALU.mult))
                chain.link(vec.tensor_scalar(g2[:], g1[:], -2 * GELU_C * 0.044715, -2 * GELU_C, ALU.mult, ALU.add))
                chain.link(vec.tensor_tensor(g1[:], g2[:], hid[:], ALU.mult))
                vec.tensor_scalar(g3[:], g1[:], 80.0, None, ALU.min).then_inc(arg_made, 1)
                chain.link(vec.tensor_tensor(wh[:], hid[:], wgt[u][:, g, :], ALU.mult))
                vec.wait_ge(gelu_exp, t * PH + g + 1)
                chain.link(vec.tensor_scalar(g2[:], g4[:], 1.0, None, ALU.add))
                chain.link(vec.reciprocal(g2[:], g2[:]))
                wait_count(vec, diag_made, t * NSLOT + g * TOPK)
                vec.tensor_tensor(coef[:], wh[:], g2[:], ALU.mult).then_inc(coef_made, 1)
                assert chain.n == start + GROUP_LINKS

            def finish(t, u):
                vec.wait_ge(diag_used, t * PH + PH + RG)
                wait_count(vec, y_out, t * 16)
                vec.tensor_tensor(yo[:], acc[u][:], x2[u][:], ALU.add).then_inc(y_made, 1)

            def tile(t, u, chain, routes=True):
                for g in range(PH):
                    group(t, u, g, chain)
                    if g == 3 and routes:
                        route(t + 1, 1 - u, chain)
                finish(t, u)

            route(0, 0, chain)
            base = chain.n
            for u in range(2):
                tile(u, u, chain)
            with vec.Fori(1, NT // 2 - 1) as r:
                chain = Chain(vec, dve, r * (2 * TILE_LINKS) + base)
                for u in range(2):
                    tile(r * 2 + u, u, chain)
            chain = Chain(vec, dve, (NT - 2) * TILE_LINKS + base)
            tile(NT - 2, 0, chain)
            tile(NT - 1, 1, chain, routes=False)


def program(nc, x, ctx_t, w_q, w_kv, w_proj, w_rel, f_wq, gamma_t, beta_t, keys_t, table, ident, out):
    with ExitStack() as ctx:
        def dram(name, shape):
            return nc.dram_tensor(name, shape, F32, kind="Internal").ap()

        qa_d = dram("qa_d", [2, NHEAD * DH, TQ])
        ka_d = dram("ka_d", [2, NHEAD * DH, TK])
        bq_d = dram("bq_d", [MAX0 - BIAS0, H, TQ])
        kc_d = dram("kc_d", [KROWS - BIAS0, TK])
        m_d = dram("m_d", [4, 2, TQ])
        x2_d = dram("x2_d", [B * TQ, D])
        xn_d = dram("xn_d", [B * TQ, D])
        q_d = dram("q_d", [NT, P, QC, P])
        mvq = ctx.enter_context(nc.sbuf_tensor("mvq", [P, QC, 2], F32))
        with ExitStack() as attention:
            ao = attention.enter_context(nc.sbuf_tensor("ao", [P, NHEAD, QT, DH], F32))
            with ExitStack() as values:
                v_all = values.enter_context(nc.sbuf_tensor("v_all", [P, NHEAD, KT, DH], F32))
                project(nc, x, ctx_t, w_q, w_kv, w_rel, ident, qa_d, ka_d, bq_d, kc_d, v_all, ao)
                attend(nc, qa_d, ka_d, bq_d, kc_d, m_d, v_all, ao, ident)
            mix(nc, x, w_proj, f_wq, ident, ao, x2_d, xn_d, q_d, mvq)
        experts(nc, table, keys_t, gamma_t, beta_t, ident, mvq, x2_d, xn_d, q_d, out)


def kernel(**inputs):
    import numpy as np
    import concourse.bacc as bacc
    from concourse.bass_utils import run_bass_kernel_spmd

    a = {k: np.asarray(v) for k, v in inputs.items()}
    c = np.ascontiguousarray
    arrays = {
        "x": a["x"],
        "ctx_t": c(a["ctx_1024"].reshape(B * TK, D).T),
        "w_q": a["L0_xattn_w_q"],
        "w_kv": a["L0_xattn_w_kv"],
        "w_proj": a["L0_xattn_w_proj"],
        "w_rel": a["L0_xattn_w_rel"],
        "f_wq": a["L0_ffn_w_q"],
        "gamma_t": c(a["L0_ffn_bn_gamma"].reshape(QC, P).T),
        "beta_t": c(a["L0_ffn_bn_beta"].reshape(QC, P).T),
        "keys_t": c(a["L0_ffn_keys"].transpose(3, 2, 0, 1).reshape(KD, QC, NKEY)),
        "table": np.concatenate([a["L0_ffn_down_embed"], a["L0_ffn_up_embed"]], axis=1),
        "ident": np.eye(P, dtype=np.float32),
    }
    nc = bacc.Bacc("TRN2", target_bir_lowering=False, num_devices=1)
    aps = [nc.dram_tensor(n, v.shape, mybir.dt.from_np(v.dtype), kind="ExternalInput").ap() for n, v in arrays.items()]
    out = nc.dram_tensor("out", [B * TQ, D], F32, kind="ExternalOutput").ap()
    program(nc, *aps, out)
    r = run_bass_kernel_spmd(nc, [arrays], core_ids=[0])
    return r.results[0]["out"].reshape(B, TQ, D)
```
